# Optimizing a Trainium2 kernel written in Bass

```python
import numpy as np
import jax
import jax.numpy as jnp

def _softmax(x, axis=-1):
    return jax.nn.softmax(x, axis=axis)

def _gelu(x):
    return jax.nn.gelu(x, approximate=True)

def _silu(x):
    return jax.nn.silu(x)

def _sigmoid(x):
    return jax.nn.sigmoid(x)

def _layernorm(x, axis=-1, eps=1e-05):
    m = jnp.mean(x, axis=axis, keepdims=True)
    v = jnp.var(x, axis=axis, keepdims=True)
    return (x - m) / jnp.sqrt(v + eps)

def _scatter_add(tgt, idx, src, axis=0):
    return tgt.at[idx].add(src)

def _segment_sum(src, seg, n):
    return jax.ops.segment_sum(src, seg, n)
kernel_name = 'mk_xattn_ffn_d1_seqx_r8_1989bd'

def setup_inputs(seed: int=0):
    np.random.seed(seed)
    _w = jnp.asarray

    def _rec_inputs():
        import jax
        import jax.numpy as jnp
        _rk = jax.random.key(seed)
        x = 7.22e-05 + 1 * jax.random.normal(jax.random.fold_in(_rk, 1), (4, 256, 256), jnp.float32)
        _lenS = 256 - jax.random.randint(jax.random.fold_in(_rk, 7), (4,), 0, max(1, 256 // 4) + 1, jnp.int32)
        _lenS2 = 256 - jax.random.randint(jax.random.fold_in(_rk, 8), (4,), 0, max(1, 256 // 4) + 1, jnp.int32)
        _ctx_2048P = jax.random.normal(jax.random.fold_in(_rk, 11), (4, 16, 256), jnp.float32)
        _ctx_2048c = jax.random.dirichlet(jax.random.fold_in(_rk, 511), 0.3 * jnp.ones((16,), jnp.float32), (4, 256))
        _ctx_2048t = jnp.einsum('bsk,bkd->bsd', _ctx_2048c, _ctx_2048P)
        _ctx_2048t = _ctx_2048t * jax.lax.rsqrt(jnp.mean(jnp.square(_ctx_2048t)) + 1e-12) * 0.953939
        ctx_2048 = 4.13588e-05 + 0.999923 * (_ctx_2048t + 0.3 * jax.random.normal(jax.random.fold_in(_rk, 611), (4, 256, 256), jnp.float32))
        return (x, ctx_2048)
    x, ctx_2048 = _rec_inputs()

    def _L0_xattn_setup():
        import math
        import jax, jax.numpy as jnp
        import numpy as np
        HEADS = 16
        MASKED_BIAS = -10000.0

        def _mha(q, k, v):
            B, Sq, D = q.shape
            Sk = k.shape[-2]
            hd = D // HEADS
            qh = q.reshape(B, Sq, HEADS, hd).transpose(0, 2, 1, 3)
            kh = k.reshape(B, Sk, HEADS, hd).transpose(0, 2, 1, 3)
            vh = v.reshape(B, Sk, HEADS, hd).transpose(0, 2, 1, 3)
            scores = jnp.einsum('bhqd,bhkd->bhqk', qh, kh) / math.sqrt(hd)
            qi = jnp.arange(Sq)[:, None] + (Sk - Sq)
            ki = jnp.arange(Sk)[None, :]
            causal = ki <= qi
            scores = jnp.where(causal[None, None], scores, jnp.asarray(MASKED_BIAS, scores.dtype))
            attn = jax.nn.softmax(scores, axis=-1)
            out = jnp.einsum('bhqk,bhkd->bhqd', attn, vh)
            return out.transpose(0, 2, 1, 3).reshape(B, Sq, D)
        key = jax.random.key(seed)
        kq, kk, kv = jax.random.split(key, 3)
        B, S, D = (4, 128, 256)
        q = jax.random.normal(kq, (B, S, D), dtype=jnp.float32)
        k = jax.random.normal(kk, (B, S, D), dtype=jnp.float32)
        v = jax.random.normal(kv, (B, S, D), dtype=jnp.float32)
        return {'q': q, 'k': k, 'v': v}
    _L0_xattn_all = _L0_xattn_setup()
    _L0_xattn_in = {k: v for k, v in _L0_xattn_all.items() if k in ()}
    del _L0_xattn_all

    def _L0_ffn_setup():
        import jax, jax.numpy as jnp
        import numpy as np
        ALPHA = 1.702
        LIMIT = 7.0
        TOP_K = 4
        B, S, H = (1, 128, 256)
        E, D = (16, 256)
        key = jax.random.key(seed)
        ks = jax.random.split(key, 7)
        s = 0.02
        return {'hidden_states': jax.random.normal(ks[0], (B, S, H), dtype=jnp.float32), 'router_weight': jax.random.normal(ks[1], (E, H), dtype=jnp.float32) * s, 'router_bias': jax.random.normal(ks[2], (E,), dtype=jnp.float32) * s, 'gate_up_proj': jax.random.normal(ks[3], (E, H, 2 * D), dtype=jnp.float32) * s, 'gate_up_proj_bias': jax.random.normal(ks[4], (E, 2 * D), dtype=jnp.float32) * s, 'down_proj': jax.random.normal(ks[5], (E, D, H), dtype=jnp.float32) * s, 'down_proj_bias': jax.random.normal(ks[6], (E, H), dtype=jnp.float32) * s}
    _L0_ffn_all = _L0_ffn_setup()
    _L0_ffn_in = {k: v for k, v in _L0_ffn_all.items() if k in ('router_weight', 'router_bias', 'gate_up_proj', 'gate_up_proj_bias', 'down_proj', 'down_proj_bias')}
    del _L0_ffn_all
    return {'x': x, 'ctx_2048': ctx_2048, 'L0_ffn_router_weight': _L0_ffn_in['router_weight'], 'L0_ffn_router_bias': _L0_ffn_in['router_bias'], 'L0_ffn_gate_up_proj': _L0_ffn_in['gate_up_proj'], 'L0_ffn_gate_up_proj_bias': _L0_ffn_in['gate_up_proj_bias'], 'L0_ffn_down_proj': _L0_ffn_in['down_proj'], 'L0_ffn_down_proj_bias': _L0_ffn_in['down_proj_bias']}

def reference(x, ctx_2048, L0_ffn_router_weight, L0_ffn_router_bias, L0_ffn_gate_up_proj, L0_ffn_gate_up_proj_bias, L0_ffn_down_proj, L0_ffn_down_proj_bias):
    import jax
    import jax.numpy as jnp

    def _L0_xattn_ref(q, k, v):
        import math
        import jax, jax.numpy as jnp
        import numpy as np
        HEADS = 16
        MASKED_BIAS = -10000.0

        def _mha(q, k, v):
            B, Sq, D = q.shape
            Sk = k.shape[-2]
            hd = D // HEADS
            qh = q.reshape(B, Sq, HEADS, hd).transpose(0, 2, 1, 3)
            kh = k.reshape(B, Sk, HEADS, hd).transpose(0, 2, 1, 3)
            vh = v.reshape(B, Sk, HEADS, hd).transpose(0, 2, 1, 3)
            scores = jnp.einsum('bhqd,bhkd->bhqk', qh, kh) / math.sqrt(hd)
            qi = jnp.arange(Sq)[:, None] + (Sk - Sq)
            ki = jnp.arange(Sk)[None, :]
            causal = ki <= qi
            scores = jnp.where(causal[None, None], scores, jnp.asarray(MASKED_BIAS, scores.dtype))
            attn = jax.nn.softmax(scores, axis=-1)
            out = jnp.einsum('bhqk,bhkd->bhqd', attn, vh)
            return out.transpose(0, 2, 1, 3).reshape(B, Sq, D)
        return _mha(q, k, v)

    def _L0_ffn_ref(hidden_states, router_weight, router_bias, gate_up_proj, gate_up_proj_bias, down_proj, down_proj_bias):
        import jax, jax.numpy as jnp
        import numpy as np
        ALPHA = 1.702
        LIMIT = 7.0
        TOP_K = 4
        B, S, H = (1, 128, 256)
        E, D = (16, 256)
        batch, seq, hdim = hidden_states.shape
        x = hidden_states.reshape(-1, hdim)
        T = x.shape[0]
        logits = x @ router_weight.T + router_bias
        top_val, top_idx = jax.lax.top_k(logits, TOP_K)
        top_val = jax.nn.softmax(top_val, axis=-1)
        router_scores = jnp.zeros_like(logits).at[jnp.arange(T)[:, None], top_idx].set(top_val)
        gate_up = jnp.einsum('th,ehd->etd', x, gate_up_proj) + gate_up_proj_bias[:, None, :]
        gate = gate_up[..., ::2]
        up = gate_up[..., 1::2]
        gate = jnp.minimum(gate, LIMIT)
        up = jnp.clip(up, -LIMIT, LIMIT)
        glu = gate * jax.nn.sigmoid(gate * ALPHA)
        out = jnp.einsum('etd,edh->eth', (up + 1.0) * glu, down_proj) + down_proj_bias[:, None, :]
        out = out * router_scores.T[:, :, None]
        out = out.sum(axis=0)
        return out.reshape(batch, seq, hdim)
    x = x + _L0_xattn_ref(_layernorm(x, axis=-1), ctx_2048, ctx_2048)
    x = x + _L0_ffn_ref(_layernorm(x, axis=-1), L0_ffn_router_weight, L0_ffn_router_bias, L0_ffn_gate_up_proj, L0_ffn_gate_up_proj_bias, L0_ffn_down_proj, L0_ffn_down_proj_bias)
    return x

_drawn_inputs = setup_inputs


def setup_inputs(seed=0):
    import zlib

    import numpy as np

    out = dict(_drawn_inputs(seed))
    spreads = {}
    factors = {'L0_ffn_router_weight': 2.729,
     'L0_ffn_router_bias': 25.256,
     'L0_ffn_gate_up_proj_bias': 33.054,
     'L0_ffn_down_proj_bias': 7.281}
    for name, (base, spread) in spreads.items():
        noise = np.random.default_rng([zlib.crc32(name.encode()), seed]).standard_normal(out[name].shape)
        drawn = base * np.exp(spread * noise) if base else spread * noise
        out[name] = jnp.asarray(drawn.astype(out[name].dtype))
    for name, factor in factors.items():
        out[name] = (out[name] * factor).astype(out[name].dtype)
    return out
```

```python
from contextlib import ExitStack

import concourse.bass as bass
from concourse import mybir

F32 = mybir.dt.float32
F32R = mybir.dt.float32r
BF16 = mybir.dt.bfloat16
U32 = mybir.dt.uint32
ALU = mybir.AluOpType
ACT = mybir.ActivationFunctionType
AX = mybir.AxisListType

P = 128
NEG = -1.0e30
EPS = 1e-5
ALPHA = 1.702
LIMIT = 7.0
TOP_K = 4


def xattn_moe(nc, x, ctx_in, w_router, b_router, w_gu, b_gu, w_dn, b_dn, score_dram, out):
    B, S, D = x.shape
    E = w_router.shape[0]
    H = 16
    HD = D // H
    PAIRS = H // 2
    T = B * S
    NT = T // P
    TB = S // P
    KD = D // P
    F = w_dn.shape[1]
    FD = F // P
    SC = 1.0 / HD ** 0.5
    ST = 64
    GRP = 512
    NG = T // GRP
    CH = NG * FD
    UNITS = 6
    ST_RING, P_RING = 4, 12
    assert (B, TB, KD, FD, NG) == (4, 2, 2, 2, 2)

    with ExitStack() as es:
        def sb(name, shape, dt=F32):
            return es.enter_context(nc.sbuf_tensor(name, shape, dt))

        def sem(name):
            return es.enter_context(nc.semaphore(name))

        ps = es.enter_context(nc.psum_tensor("ps", [P, 8, 512], F32))
        WORK, PVB = 4, 6

        ident = sb("ident", [P, P])
        ident_b = sb("ident_b", [P, P], BF16)
        mask_q0 = sb("mask_q0", [P, 4, P], BF16)
        mask_q1 = sb("mask_q1", [P, 2, S], BF16)
        iota_e = sb("iota_e", [P, E])
        eps_col = sb("eps_col", [P, 1])

        x_tok = sb("x_tok", [P, NT, D])
        ctx_tok = sb("ctx_tok", [P, NT, D])
        stats = sb("stats", [P, NT, 6])
        mv = sb("mv", [P, NT, 2])
        std = sb("std", [P, NT])
        rstd = sb("rstd", [P, NT])
        shift = sb("shift", [P, NT])
        q_norm = sb("q_norm", [P, 2, TB, D])
        q_stack = sb("q_stack", [P, 2, TB, H, ST], F32R)
        k_stack = sb("k_stack", [P, 2, TB, H, ST], F32R)
        q_t = sb("q_t", [P, 2, PAIRS, S], F32R)
        k_t = sb("k_t", [P, 2, PAIRS, S], F32R)
        v_aug = sb("v_aug", [P, 2, TB, H, 32])
        neg_max = sb("neg_max", [P, 2, TB, 2, PAIRS])
        max_t = sb("max_t", [H, 2, S], F32R)
        prob = sb("prob", [P, P_RING, 512])
        o_t = sb("o_t", [P, 4, S])
        r_den = sb("r_den", [P, H])
        attn = sb("attn", [P, D])

        y = ctx_tok
        y_hi = k_t[:, 0, :, :].rearrange("p (k a) s -> p k (a s)", k=KD)
        y_lo = k_t[:, 1, :, :].rearrange("p (k a) s -> p k (a s)", k=KD)
        wr_sb = sb("wr_sb", [E, D])
        br_sb = sb("br_sb", [P, E])
        wr_t = sb("wr_t", [P, KD, 2 * E], F32R)
        bgu_sb = sb("bgu_sb", [E, 2 * F])
        bias_g = sb("bias_g", [P, FD, E])
        bias_u = sb("bias_u", [P, FD, E])
        bdn_sb = sb("bdn_sb", [E, D])
        lg2 = sb("lg2", [P, NT, 2 * E])
        logits = sb("logits", [P, NT, E])
        top8 = sb("top8", [P, NT, 8])
        idx8 = sb("idx8", [P, NT, 8], U32)
        idx_f = sb("idx_f", [P, NT, TOP_K])
        top_d = sb("top_d", [P, NT, TOP_K])
        top_e = sb("top_e", [P, NT, TOP_K])
        top_s = sb("top_s", [P, NT])
        top_r = sb("top_r", [P, NT])
        top_w = sb("top_w", [P, NT, TOP_K])
        onehot = sb("onehot", [P, NT * TOP_K, E])
        onehot_w = sb("onehot_w", [P, NT * TOP_K, E])
        score = sb("score", [P, NT, E])
        score_t = sb("score_t", [E, T])
        score_b = sb("score_b", [P, 2, T])

        raw_gu = sb("raw_gu", [P, 2, KD, 2 * F])
        raw_dn = sb("raw_dn", [P, 2, FD, D])
        gu_hi = sb("gu_hi", [P, 2, KD, 2, F], F32R)
        gu_lo = sb("gu_lo", [P, 2, KD, 2, F], F32R)
        dn_hi = sb("dn_hi", [P, 2, FD, D], F32R)
        dn_lo = sb("dn_lo", [P, 2, FD, D], F32R)
        hid, gate, sig = prob[:, 0:4, :], prob[:, 4:6, :], prob[:, 6:8, :]
        glu, up = prob[:, 8:10, :], prob[:, 10:12, :]
        out_t = prob[:, 0:8, :].rearrange("p (g k) t -> p g k t", k=KD)
        out_sb = prob[:, 8:12, :].rearrange("p j (a d) -> p (j a) d", d=D)
        up_s = sb("up_s", [P, 2, GRP])
        h_hi = q_t[:, 0, :, :].rearrange("p (c a) s -> p c (a s)", c=CH)
        h_lo = q_t[:, 1, :, :].rearrange("p (c a) s -> p c (a s)", c=CH)

        x_in = [sem(f"x_in{b}") for b in range(B)]
        ctx_dma = [sem(f"ctx_in{b}") for b in range(B)]
        small_in = sem("small_in")
        consts = sem("consts")
        pool_step = sem("pool_step")
        dve_step = sem("dve_step")
        var1 = sem("var1")
        std1 = sem("std1")
        small_t = sem("small_t")
        small_done = sem("small_done")
        stack_hi = sem("stack_hi")
        stack_dup = sem("stack_dup")
        stack_lo = sem("stack_lo")
        v_ready = sem("v_ready")
        work_full = sem("work_full")
        work_act = sem("work_act")
        work_dve = sem("work_dve")
        max_t_ready = sem("max_t_ready")
        max_rows = [sem("max_rows0"), sem("max_rows1")]
        st_full = sem("st_full")
        exp_done = sem("exp_done")
        sel_done = sem("sel_done")
        pv_done = sem("pv_done")
        o_evac = sem("o_evac")
        var2 = sem("var2")
        std2 = sem("std2")
        y_ready = sem("y_ready")
        yt_full = sem("yt_full")
        yhi_ready = sem("yhi_ready")
        ylo_ready = sem("ylo_ready")
        lg_full = sem("lg_full")
        lg_copied = sem("lg_copied")
        topd_ready = sem("topd_ready")
        tope_ready = sem("tope_ready")
        score_ready = sem("score_ready")
        score_tr = sem("score_tr")
        score_t_ready = sem("score_t_ready")
        score_out = sem("score_out")
        score_in = [sem("score_in0"), sem("score_in1")]
        raw_in = [sem("raw_in0"), sem("raw_in1")]
        w_hi = sem("w_hi")
        w_lo = sem("w_lo")
        gu_done = sem("gu_done")
        g_ready = sem("g_ready")
        u_ready = sem("u_ready")
        us_ready = sem("us_ready")
        sig_ready = sem("sig_ready")
        glu_ready = sem("glu_ready")
        h_ready = sem("h_ready")
        hhi_ready = sem("hhi_ready")
        hlo_ready = sem("hlo_ready")
        dn_done = sem("dn_done")
        outt_ready = [sem("outt_act"), sem("outt_dve")]
        out_tr = sem("out_tr")
        out_ready = sem("out_ready")
        out_dma = sem("out_dma")

        def fwait(eng, s, n):
            if not isinstance(n, int) or n > 0:
                eng.wait_ge(s, n)

        uses = []

        def plan_t(b):
            uses.extend(("T", b, n) for n in range(8))

        def plan_x(b):
            uses.extend(("X", b, n) for n in range(12))

        plan_t(0)
        plan_x(0)
        uses.append(("M", 0, 0))
        for b in range(B):
            if b + 1 < B:
                plan_t(b + 1)
                plan_x(b + 1)
                uses.append(("M", b + 1, 0))
            uses.extend(("O", b, t) for t in range(TB))
        slot_of = {u: i for i, u in enumerate(uses)}
        emptied = []
        n_act = n_dve = 0
        for kind, _, _ in uses:
            if kind == "T":
                n_act += 1
                emptied.append((work_act, n_act))
            else:
                n_dve += 1
                emptied.append((work_dve, n_dve))
        work_dve_total, work_act_total = n_dve, n_act

        def work_bank(use):
            return WORK + slot_of[use] % 2

        def t_use(n):
            return n // 4, (n // 2) % 2, n % 2

        def x_use(n):
            if n < 4:
                return 0, n // 2, 4 * (n % 2), 4, P
            n -= 4
            return 1, n // 4, 2 * (n % 4), 2, S

        def st_unit(i):
            if i < 4:
                return i % 2, 2 * (i // 2), 2, 0, 0
            return i % 2, 0, 4, 1, P

        block = es.enter_context(nc.Block())

        @block.sync
        def _(sp):
            def load_weights(e, par):
                sp.dma_start(raw_gu[:, par, :, :], w_gu[e].rearrange("(k p) n -> p k n", p=P)
                             ).then_inc(raw_in[par], 16)
                sp.dma_start(raw_dn[:, par, :, :], w_dn[e].rearrange("(k p) n -> p k n", p=P)
                             ).then_inc(raw_in[par], 16)

            def load_scores(e, par):
                sp.dma_start(score_b[:, par, :], score_dram[e, :].partition_broadcast(P)
                             ).then_inc(score_in[par], 16)

            for b in range(B):
                sp.dma_start(x_tok[:, TB * b:TB * b + TB, :], x[b].rearrange("(t p) d -> p t d", p=P)
                             ).then_inc(x_in[b], 16)
            load_weights(0, 0)
            load_weights(1, 1)
            for b in range(B):
                sp.wait_ge(max_t_ready, b + 1)
                for s in range(2):
                    sp.dma_start(q_t[64 * s + 32:64 * s + 33, b % 2, :, :].bitcast(F32),
                                 max_t[PAIRS * s:PAIRS * (s + 1), b % 2, :].bitcast(F32)
                                 ).then_inc(max_rows[b % 2], 16)
            sp.wait_ge(score_t_ready, 2)
            sp.dma_start(score_dram[:, :], score_t[:, :]).then_inc(score_out, 16)
            sp.wait_ge(score_out, 16)
            load_scores(0, 0)
            load_scores(1, 1)
            with sp.Fori(0, E // 2 - 1) as i:
                for par in range(2):
                    e = 2 * i + par
                    sp.wait_ge(w_hi, 2 * e + 2)
                    sp.wait_ge(w_lo, 3 * e + 3)
                    load_weights(e + 2, par)
                    sp.wait_ge(us_ready, CH * e + CH)
                    load_scores(e + 2, par)
            for j in range(4):
                sp.wait_ge(out_ready, j + 1)
                sp.dma_start(out[j].rearrange("(t p) d -> p t d", p=P), out_sb[:, 2 * j:2 * j + 2, :]
                             ).then_inc(out_dma, 16)
            sp.wait_ge(out_dma, 64)

        @block.gpsimd
        def _(pool):
            done = [0]

            def step(ins):
                done[0] += 1
                ins.then_inc(pool_step, 1)

            def settle():
                pool.wait_ge(pool_step, done[0])

            step(pool.memset(ident[:, :], 0.0))
            step(pool.memset(ident_b[:, :], 0.0))
            step(pool.memset(mask_q0[:, :, :], 0.0))
            step(pool.memset(mask_q1[:, :, :], 0.0))
            pool.memset(eps_col[:, :], EPS).then_inc(consts, 1)
            settle()
            for m in (ident, ident_b):
                pool.affine_select(out=m[:, :], in_=m[:, :], compare_op=ALU.not_equal, fill=1.0, base=0,
                                   pattern=[[-1, P]], channel_multiplier=1).then_inc(consts, 1)
            pool.affine_select(out=mask_q0[:, :, :], in_=mask_q0[:, :, :], compare_op=ALU.is_ge, fill=NEG,
                               base=0, pattern=[[0, 4], [-1, P]], channel_multiplier=1).then_inc(consts, 1)
            pool.affine_select(out=mask_q1[:, :, :], in_=mask_q1[:, :, :], compare_op=ALU.is_ge, fill=NEG,
                               base=P, pattern=[[0, 2], [-1, S]], channel_multiplier=1).then_inc(consts, 1)
            for par in range(2):
                for t in range(TB):
                    pool.memset(q_stack[:, par, t, :, 32:48].bitcast(F32), 0.0).then_inc(consts, 1)
                    pool.memset(k_stack[:, par, t, :, 32:33].bitcast(F32), 1.0).then_inc(consts, 1)
                    pool.memset(k_stack[:, par, t, :, 33:48].bitcast(F32), 0.0).then_inc(consts, 1)
                    pool.memset(v_aug[:, par, t, :, HD:HD + 1], 1.0).then_inc(consts, 1)
                    pool.memset(v_aug[:, par, t, :, HD + 1:32], 0.0).then_inc(consts, 1)
            pool.iota(iota_e[:, :], pattern=[[1, E]], base=0, channel_multiplier=0,
                      allow_small_or_imprecise_dtypes=True).then_inc(consts, 1)

            def values(b):
                pool.wait_ge(ctx_dma[b], 16)
                if b >= 2:
                    pool.wait_ge(pv_done, 4 * (b - 1))
                for t in range(TB):
                    pool.tensor_scalar(v_aug[:, b % 2, t, :, 0:HD],
                                       ctx_tok[:, TB * b + t, :].rearrange("p (h d) -> p h d", h=H),
                                       1.0, None, ALU.mult).then_inc(v_ready, 1)

            def lo_gu(e, par, k):
                pool.wait_ge(w_hi, 2 * e + 1)
                pool.tensor_tensor(gu_lo[:, par, k, :, :],
                                   raw_gu[:, par, k, :].rearrange("p (d g) -> p g d", g=2),
                                   gu_hi[:, par, k, :, :].bitcast(F32), ALU.subtract).then_inc(w_lo, 1)

            def lo_dn(e, par):
                pool.wait_ge(w_hi, 2 * e + 2)
                pool.tensor_tensor(dn_lo[:, par, :, :], raw_dn[:, par, :, :],
                                   dn_hi[:, par, :, :].bitcast(F32), ALU.subtract).then_inc(w_lo, 1)

            values(0)
            values(1)
            for sg in range(2 * B):
                for i in range(UNITS):
                    u = sg * UNITS + i
                    pool.wait_ge(exp_done, u + 1)
                    if i < 4:
                        blk = prob[:, u % P_RING, :].rearrange("p (h q) -> p h q", q=S)[:, :, 0:P]
                        n = 2
                    else:
                        blk = prob[:, u % P_RING, :].rearrange("p (h q) -> p h q", q=P)
                        n = 4
                    pool.affine_select(out=blk, in_=blk, compare_op=ALU.is_ge, fill=0.0, base=0,
                                       pattern=[[0, n], [1, P]], channel_multiplier=-1).then_inc(sel_done, 1)
                if sg % 2 and sg // 2 + 2 < B:
                    values(sg // 2 + 2)
                if sg == 0:
                    lo_gu(0, 0, 0)
                    lo_gu(0, 0, 1)
                    lo_dn(0, 0)

            def expert(e, par, last):
                for c in range(CH):
                    n = CH * e + c
                    pool.wait_ge(sig_ready, n + 1)
                    fwait(pool, h_ready, n - 1)
                    pool.tensor_tensor(glu[:, c % 2, :], gate[:, c % 2, :], sig[:, c % 2, :],
                                       ALU.mult).then_inc(glu_ready, 1)
                    if not last and c < 2:
                        lo_gu(e + 1, 1 - par, c)
                    if not last and c == 2:
                        lo_dn(e + 1, 1 - par)

            expert(0, 0, False)
            expert(1, 1, False)
            with pool.Fori(1, E // 2 - 1) as i:
                expert(2 * i, 0, False)
                expert(2 * i + 1, 1, False)
            expert(E - 2, 0, False)
            expert(E - 1, 1, True)

        @block.scalar
        def _(act):
            for b in range(B):
                act.dma_start(ctx_tok[:, TB * b:TB * b + TB, :], ctx_in[b].rearrange("(t p) d -> p t d", p=P)
                              ).then_inc(ctx_dma[b], 16)
            act.dma_start(wr_sb[:, :], w_router[:, :]).then_inc(small_in, 16)
            act.dma_start(bgu_sb[:, :], b_gu[:, :]).then_inc(small_in, 16)
            act.dma_start(bdn_sb[:, :], b_dn[:, :]).then_inc(small_in, 16)
            act.dma_start(br_sb[:, :], b_router.partition_broadcast(P)).then_inc(small_in, 16)
            act.wait_ge(consts, 1)
            act.wait_ge(var1, 1)
            act.activation(std[:, :], mv[:, :, 1], ACT.Sqrt, bias=eps_col[:, :]).then_inc(std1, 1)

            def dup(b):
                par = b % 2
                act.wait_ge(stack_hi, 2 * b + 2)
                if b >= 2:
                    act.wait_ge(work_full, slot_of[("T", b - 2, 7)] + 1)
                for t in range(TB):
                    act.activation(q_stack[:, par, t, :, 48:64], q_stack[:, par, t, :, 0:16].bitcast(F32),
                                   ACT.Copy).then_inc(stack_dup, 1)
                    act.activation(k_stack[:, par, t, :, 16:32], k_stack[:, par, t, :, 0:16].bitcast(F32),
                                   ACT.Copy).then_inc(stack_dup, 1)

            def evac_t(b):
                for n in range(8):
                    t, half, which = t_use(n)
                    u = ("T", b, n)
                    act.wait_ge(work_full, slot_of[u] + 1)
                    if b >= 2:
                        act.wait_ge(st_full, 2 * UNITS * (b - 1))
                    dst = (q_t, k_t)[which]
                    act.activation(dst[:, b % 2, 4 * half:4 * half + 4, t * P:(t + 1) * P],
                                   ps[:, work_bank(u), :].rearrange("p (a q) -> p a q", a=4),
                                   ACT.Copy).then_inc(work_act, 1)

            def exps(sg):
                for i in range(UNITS):
                    u = sg * UNITS + i
                    act.wait_ge(st_full, u + 1)
                    if u >= P_RING:
                        act.wait_ge(pv_done, 2 * (sg - 1))
                    act.activation(prob[:, u % P_RING, :], ps[:, u % ST_RING, :], ACT.Exp,
                                   scale=SC).then_inc(exp_done, 1)

            def split_gu(e, par):
                act.activation(gu_hi[:, par, :, :, :], raw_gu[:, par, :, :].rearrange("p k (d g) -> p k g d", g=2),
                               ACT.Copy).then_inc(w_hi, 1)

            def split_dn(e, par):
                act.activation(dn_hi[:, par, :, :], raw_dn[:, par, :, :], ACT.Copy).then_inc(w_hi, 1)

            dup(0)
            evac_t(0)
            dup(1)
            for b in range(B):
                exps(2 * b)
                if b + 1 < B:
                    evac_t(b + 1)
                if b == 0:
                    act.wait_ge(raw_in[0], 32)
                    split_gu(0, 0)
                    split_dn(0, 0)
                exps(2 * b + 1)
                if b + 2 < B:
                    dup(b + 2)
            act.wait_ge(var2, 1)
            act.activation(std[:, :], mv[:, :, 1], ACT.Sqrt, bias=eps_col[:, :]).then_inc(std2, 1)
            for j in range(4):
                tg, k = j // 2, j % 2
                act.wait_ge(yt_full, j + 1)
                act.activation(y_hi[:, k, tg * GRP:(tg + 1) * GRP], ps[:, j, :], ACT.Copy).then_inc(yhi_ready, 1)
            act.wait_ge(topd_ready, 1)
            act.activation(top_e[:, :, :], top_d[:, :, :], ACT.Exp).then_inc(tope_ready, 1)

            def high_half(n, c):
                act.wait_ge(h_ready, n + 1)
                fwait(act, dn_done, n - 3)
                act.activation(h_hi[:, c, :], hid[:, c, :], ACT.Copy).then_inc(hhi_ready, 1)

            def expert(e, par, first, last):
                for c in range(CH):
                    n = CH * e + c
                    act.wait_ge(g_ready, n + 1)
                    fwait(act, glu_ready, n - 1)
                    act.activation(sig[:, c % 2, :], gate[:, c % 2, :], ACT.Sigmoid, scale=ALPHA
                                   ).then_inc(sig_ready, 1)
                    if not (first and c == 0):
                        high_half(n - 1, (c - 1) % CH)
                    if not last and c == 0:
                        act.wait_ge(raw_in[1 - par], 16 * (e + par) + 32)
                        if not first:
                            act.wait_ge(gu_done, CH * e)
                        split_gu(e + 1, 1 - par)
                    if not last and c == 2:
                        if not first:
                            act.wait_ge(dn_done, CH * e)
                        split_dn(e + 1, 1 - par)

            expert(0, 0, True, False)
            expert(1, 1, False, False)
            with act.Fori(1, E // 2 - 1) as i:
                expert(2 * i, 0, False, False)
                expert(2 * i + 1, 1, False, False)
            expert(E - 2, 0, False, False)
            expert(E - 1, 1, False, True)
            high_half(CH * E - 1, CH - 1)
            for tg in range(NG):
                act.wait_ge(dn_done, CH * E)
                act.activation(out_t[:, tg, 0, :], ps[:, 4 + 2 * tg, :], ACT.Copy).then_inc(outt_ready[0], 1)

        @block.vector
        def _(dve):
            done = [0]

            def step(ins):
                done[0] += 1
                ins.then_inc(dve_step, 1)

            def settle():
                dve.wait_ge(dve_step, done[0])

            def norm_scale():
                step(dve.reciprocal(rstd[:, :], std[:, :]))
                settle()
                step(dve.scalar_tensor_tensor(shift[:, :], mv[:, :, 0], -1.0, rstd[:, :], ALU.mult, ALU.mult))
                settle()

            for b in range(B):
                dve.wait_ge(x_in[b], 16)
                for t in range(TB):
                    step(dve.bn_stats(stats[:, TB * b + t, :], x_tok[:, TB * b + t, :]))
            settle()
            for i in range(NT):
                ins = dve.bn_aggr(mv[:, i, :], stats[:, i, :])
                if i < NT - 1:
                    step(ins)
                else:
                    ins.then_inc(var1, 1)
            dve.wait_ge(std1, 1)
            dve.wait_ge(var1, 1)
            settle()
            norm_scale()

            def prep(b):
                par = b % 2
                for t in range(TB):
                    i = TB * b + t
                    step(dve.tensor_scalar(q_norm[:, par, t, :], x_tok[:, i, :], rstd[:, i:i + 1],
                                           shift[:, i:i + 1], ALU.mult, ALU.add))
                settle()
                if b >= 2:
                    dve.wait_ge(work_full, slot_of[("T", b - 2, 7)] + 1)
                dve.wait_ge(ctx_dma[b], 16)
                src_q = q_norm[:, par, :, :].rearrange("p t (h d) -> p (t h) d", h=H)
                src_k = ctx_tok[:, TB * b:TB * b + TB, :].rearrange("p t (h d) -> p (t h) d", h=H)
                qs = q_stack[:, par, :, :, :].rearrange("p t h c -> p (t h) c")
                ks = k_stack[:, par, :, :, :].rearrange("p t h c -> p (t h) c")
                dve.tensor_copy(qs[:, :, 0:16], src_q).then_inc(stack_hi, 1)
                dve.tensor_copy(ks[:, :, 0:16], src_k).then_inc(stack_hi, 1)
                dve.wait_ge(stack_hi, 2 * b + 2)
                dve.tensor_tensor(qs[:, :, 16:32], src_q, qs[:, :, 0:16].bitcast(F32), ALU.subtract
                                  ).then_inc(stack_lo, 1)
                dve.tensor_tensor(ks[:, :, 48:64], src_k, ks[:, :, 0:16].bitcast(F32), ALU.subtract
                                  ).then_inc(stack_lo, 1)

            def row_max(b):
                for n in range(12):
                    t, s, p0, np_, keys = x_use(n)
                    u = ("X", b, n)
                    dve.wait_ge(work_full, slot_of[u] + 1)
                    if b >= 2 and n == 0:
                        dve.wait_ge(work_full, slot_of[("M", b - 2, 0)] + 1)
                    dve.tensor_reduce(neg_max[:, b % 2, t, s, p0:p0 + np_],
                                      ps[:, work_bank(u), :].rearrange("p (a k) -> p a k", k=keys),
                                      AX.X, ALU.max, negate=True).then_inc(work_dve, 1)

            def max_rows_t(b):
                u = ("M", b, 0)
                dve.wait_ge(work_full, slot_of[u] + 1)
                if b >= 2:
                    dve.wait_ge(max_rows[b % 2], 32 * (b // 2))
                dve.tensor_copy(max_t[:, b % 2, :], ps[0:H, work_bank(u), 0:S]).then_inc(max_t_ready, 1)
                dve.wait_ge(max_t_ready, b + 1)
                dve.memset(r_den[0:1, 0:1], 0.0).then_inc(work_dve, 1)

            def evac_o(b, g):
                dve.wait_ge(pv_done, 4 * b + g + 1)
                if b >= 1:
                    dve.wait_ge(work_full, slot_of[("O", b - 1, TB - 1)] + 1)
                dve.tensor_copy(o_t[:, g, :], ps[:, PVB + g % 2, 0:S]).then_inc(o_evac, 1)

            def attn_out(b, t):
                u = ("O", b, t)
                i = TB * b + t
                dve.wait_ge(work_full, slot_of[u] + 1)
                settle()
                o = ps[:, work_bank(u), :].rearrange("p (h c) -> p h c", c=32)
                step(dve.reciprocal(r_den[:, :], o[:, :, HD]))
                settle()
                dve.tensor_tensor(attn[:, :].rearrange("p (h d) -> p h d", h=H), o[:, :, 0:HD],
                                  r_den[:, :].unsqueeze(2).to_broadcast([P, H, HD]), ALU.mult
                                  ).then_inc(work_dve, 1)
                dve.wait_ge(work_dve, emptied[slot_of[u]][1])
                step(dve.tensor_tensor(x_tok[:, i, :], x_tok[:, i, :], attn[:, :], ALU.add))
                settle()
                step(dve.bn_stats(stats[:, i, :], x_tok[:, i, :]))

            prep(0)
            dve.wait_ge(small_t, 1)
            wr_ps = ps[:, 7, 0:KD * E].rearrange("p (k e) -> p k e", k=KD)
            b_ps = ps[:, 7, KD * E:KD * E + 2 * FD * E].rearrange("p (g f e) -> p g f e", g=2, f=FD)
            step(dve.tensor_copy(wr_t[:, :, 0:E], wr_ps))
            settle()
            step(dve.tensor_tensor(wr_t[:, :, E:2 * E], wr_ps, wr_t[:, :, 0:E].bitcast(F32), ALU.subtract))
            step(dve.tensor_copy(bias_g[:, :, :], b_ps[:, 0, :, :]))
            step(dve.tensor_scalar(bias_u[:, :, :], b_ps[:, 1, :, :], 1.0, None, ALU.add))
            settle()
            dve.memset(r_den[0:1, 0:1], 0.0).then_inc(small_done, 1)
            dve.wait_ge(small_done, 1)
            row_max(0)
            max_rows_t(0)
            prep(1)
            for b in range(B):
                evac_o(b, 0)
                evac_o(b, 1)
                if b + 1 < B:
                    row_max(b + 1)
                evac_o(b, 2)
                if b + 1 < B:
                    max_rows_t(b + 1)
                evac_o(b, 3)
                for t in range(TB):
                    attn_out(b, t)
                if b + 2 < B:
                    prep(b + 2)
            settle()
            for i in range(NT):
                ins = dve.bn_aggr(mv[:, i, :], stats[:, i, :])
                if i < NT - 1:
                    step(ins)
                else:
                    ins.then_inc(var2, 1)
            dve.wait_ge(var2, 1)
            dve.wait_ge(std2, 1)
            settle()
            norm_scale()
            for i in range(NT):
                dve.tensor_scalar(y[:, i, :], x_tok[:, i, :], rstd[:, i:i + 1], shift[:, i:i + 1],
                                  ALU.mult, ALU.add).then_inc(y_ready, 1)
            for j in range(4):
                tg, k = j // 2, j % 2
                dve.wait_ge(yhi_ready, j + 1)
                dve.tensor_tensor(y_lo[:, k, tg * GRP:(tg + 1) * GRP], ps[:, j, :],
                                  y_hi[:, k, tg * GRP:(tg + 1) * GRP].bitcast(F32), ALU.subtract
                                  ).then_inc(ylo_ready, 1)
            dve.wait_ge(lg_full, 1)
            dve.tensor_copy(lg2[:, :, :], ps[:, WORK, 0:NT * 2 * E].rearrange("p (t c) -> p t c", t=NT)
                            ).then_inc(lg_copied, 1)
            dve.wait_ge(lg_copied, 1)
            step(dve.tensor_tensor(logits[:, :, :], lg2[:, :, 0:E], lg2[:, :, E:2 * E], ALU.add))
            settle()
            dve.wait_ge(small_in, 64)
            step(dve.tensor_tensor(logits[:, :, :], logits[:, :, :],
                                   br_sb[:, :].unsqueeze(1).to_broadcast([P, NT, E]), ALU.add))
            settle()
            for i in range(NT):
                step(dve.max(top8[:, i, :], logits[:, i, :]))
            settle()
            for i in range(NT):
                step(dve.max_index(idx8[:, i, :], top8[:, i, :], logits[:, i, :]))
            dve.tensor_tensor(top_d[:, :, :], top8[:, :, 0:TOP_K], top8[:, :, 0:1].to_broadcast([P, NT, TOP_K]),
                              ALU.subtract).then_inc(topd_ready, 1)
            settle()
            step(dve.tensor_copy(idx_f[:, :, :], idx8[:, :, 0:TOP_K]))
            settle()
            dve.wait_ge(consts, 5 + 10 * TB + 1)
            step(dve.tensor_tensor(onehot[:, :, :], iota_e[:, :].unsqueeze(1).to_broadcast([P, NT * TOP_K, E]),
                                   idx_f[:, :, :].rearrange("p t k -> p (t k)").unsqueeze(2)
                                   .to_broadcast([P, NT * TOP_K, E]), ALU.is_equal))
            dve.wait_ge(tope_ready, 1)
            step(dve.tensor_reduce(top_s[:, :], top_e[:, :, :], AX.X, ALU.add))
            settle()
            step(dve.reciprocal(top_r[:, :], top_s[:, :]))
            settle()
            step(dve.tensor_tensor(top_w[:, :, :], top_e[:, :, :],
                                   top_r[:, :].unsqueeze(2).to_broadcast([P, NT, TOP_K]), ALU.mult))
            settle()
            step(dve.tensor_tensor(onehot_w[:, :, :], onehot[:, :, :],
                                   top_w[:, :, :].rearrange("p t k -> p (t k)").unsqueeze(2)
                                   .to_broadcast([P, NT * TOP_K, E]), ALU.mult))
            settle()
            dve.tensor_reduce(score[:, :, :], onehot_w[:, :, :].rearrange("p (t k) e -> p t e k", k=TOP_K),
                              AX.X, ALU.add).then_inc(score_ready, 1)

            def low_half(n, c):
                dve.wait_ge(hhi_ready, n + 1)
                fwait(dve, dn_done, n - 3)
                dve.tensor_tensor(h_lo[:, c, :], hid[:, c, :], h_hi[:, c, :].bitcast(F32), ALU.subtract
                                  ).then_inc(hlo_ready, 1)

            def hidden(n, c):
                dve.wait_ge(glu_ready, n + 1)
                dve.wait_ge(us_ready, n + 1)
                fwait(dve, hlo_ready, n - 3)
                dve.tensor_tensor(hid[:, c, :], up_s[:, c % 2, :], glu[:, c % 2, :], ALU.mult
                                  ).then_inc(h_ready, 1)

            def expert(e, par, first, scores_copied=False):
                for c in range(CH):
                    n = CH * e + c
                    tg, f = c // FD, c % FD
                    b0 = 2 * (c % 2)
                    if not (first and c < 2):
                        low_half(n - 2, (c - 2) % CH)
                    dve.wait_ge(gu_done, n + 1)
                    fwait(dve, glu_ready, n - 1)
                    dve.tensor_scalar(gate[:, c % 2, :], ps[:, b0, :], bias_g[:, f, bass.ds(e, 1)], LIMIT,
                                      ALU.add, ALU.min).then_inc(g_ready, 1)
                    fwait(dve, us_ready, n - 1)
                    dve.tensor_scalar(up[:, c % 2, :], ps[:, b0 + 1, :], bias_u[:, f, bass.ds(e, 1)],
                                      LIMIT + 1.0, ALU.add, ALU.min).then_inc(u_ready, 1)
                    if first and c == 0:
                        for half in range(2):
                            dve.wait_ge(score_tr, half + 1)
                            dve.tensor_copy(score_t[:, half * GRP:(half + 1) * GRP], ps[0:E, 5 + half, :]
                                            ).then_inc(score_t_ready, 1)
                    dve.wait_ge(u_ready, n + 1)
                    fwait(dve, h_ready, n - 1)
                    if c == 0:
                        dve.wait_ge(score_in[par], 8 * (e - par) + 16)
                    dve.scalar_tensor_tensor(up_s[:, c % 2, :], up[:, c % 2, :], 1.0 - LIMIT,
                                             score_b[:, par, tg * GRP:(tg + 1) * GRP], ALU.max, ALU.mult
                                             ).then_inc(us_ready, 1)
                    if not (first and c == 0):
                        hidden(n - 1, (c - 1) % CH)

            expert(0, 0, True)
            expert(1, 1, False)
            with dve.Fori(1, E // 2) as i:
                expert(2 * i, 0, False)
                expert(2 * i + 1, 1, False)
            N = CH * E
            low_half(N - 2, CH - 2)
            hidden(N - 1, CH - 1)
            low_half(N - 1, CH - 1)
            for tg in range(NG):
                dve.wait_ge(dn_done, N)
                dve.tensor_copy(out_t[:, tg, 1, :], ps[:, 5 + 2 * tg, :]).then_inc(outt_ready[1], 1)
            for j in range(4):
                dve.wait_ge(out_tr, j + 1)
                dve.tensor_tensor(out_sb[:, 2 * j:2 * j + 2, :], ps[:, j, :].rearrange("p (t d) -> p t d", t=2),
                                  x_tok[:, 2 * j:2 * j + 2, :], ALU.add).then_inc(out_ready, 1)

        @block.tensor
        def _(pe):
            def claim(use):
                i = slot_of[use]
                if i >= 2:
                    pe.wait_ge(*emptied[i - 2])
                return work_bank(use)

            pe.wait_ge(consts, 5)
            pe.wait_ge(small_in, 64)
            for k in range(KD):
                pe.transpose(ps[:, 7, k * E:(k + 1) * E], wr_sb[:, k * P:(k + 1) * P], ident[0:E, 0:E])
            for g in range(2):
                for f in range(FD):
                    at = KD * E + (g * FD + f) * E
                    tr = pe.transpose(ps[:, 7, at:at + E], bgu_sb[:, 2 * f * P + g:2 * (f + 1) * P:2],
                                      ident[0:E, 0:E])
            tr.then_inc(small_t, 1)

            def stacks_t(b):
                pe.wait_ge(consts, 5 + 10 * TB)
                pe.wait_ge(stack_lo, 2 * b + 2)
                pe.wait_ge(stack_dup, 2 * TB * (b + 1))
                for n in range(8):
                    t, half, which = t_use(n)
                    bank = claim(("T", b, n))
                    src = (q_stack, k_stack)[which]
                    for j in range(4):
                        pair = 4 * half + j
                        tr = pe.transpose(ps[:, bank, j * P:(j + 1) * P],
                                          src[:, b % 2, t, 2 * pair:2 * pair + 2, :].bitcast(F32)
                                          .rearrange("p h c -> p (h c)"), ident[:, :])
                    tr.then_inc(work_full, 1)

            def row_scores(b):
                for n in range(12):
                    t, s, p0, np_, keys = x_use(n)
                    bank = claim(("X", b, n))
                    if n == 0:
                        pe.wait_ge(work_act, 8 * (b + 1))
                    mask = (mask_q0, mask_q1)[t]
                    pe.matmul(ps[:, bank, :], ident_b[:, :], mask[:, :, :].rearrange("p a k -> p (a k)"),
                              start=True, stop=True)
                    rows = slice(64 * s, 64 * s + 32)
                    for j in range(np_):
                        mm = pe.matmul(ps[:, bank, j * keys:(j + 1) * keys],
                                       q_t[rows, b % 2, p0 + j, t * P:(t + 1) * P],
                                       k_t[rows, b % 2, p0 + j, 0:keys], start=False, stop=True,
                                       skip_group_check=True)
                    mm.then_inc(work_full, 1)

            def maxima_t(b):
                bank = claim(("M", b, 0))
                pe.wait_ge(work_dve, emptied[slot_of[("X", b, 11)]][1])
                for t in range(TB):
                    tr = pe.transpose(ps[0:H, bank, t * P:(t + 1) * P],
                                      neg_max[:, b % 2, t, :, :].rearrange("p s a -> p (s a)"), ident[:, :])
                tr.then_inc(work_full, 1)

            def scores_t(b, s2):
                sg = 2 * b + s2
                if s2 == 0:
                    pe.wait_ge(max_rows[b % 2], 32 * (b // 2 + 1))
                for i in range(0, UNITS, 2):
                    u = sg * UNITS + i
                    fwait(pe, exp_done, u + 2 - ST_RING)
                    np_ = st_unit(i)[2]
                    for j in range(np_):
                        for v in range(2):
                            s, p0, _, kt, q0 = st_unit(i + v)
                            pair = 4 * s2 + p0 + j
                            w = S - q0
                            rows = slice(64 * s, 64 * s + 64)
                            mm = pe.matmul(ps[:, (u + v) % ST_RING, j * w:(j + 1) * w],
                                           k_t[rows, b % 2, pair, kt * P:(kt + 1) * P],
                                           q_t[rows, b % 2, pair, q0:S], start=True, stop=True)
                            if j == np_ - 1:
                                mm.then_inc(st_full, 1)

            def weigh(b, g):
                s2, gg = g // 2, g % 2
                sg = 2 * b + s2
                pe.wait_ge(sel_done, UNITS * (sg + 1))
                pe.wait_ge(v_ready, TB * (b + 1))
                fwait(pe, o_evac, 4 * b + g - 1)
                if b == 0 and g == 1:
                    pe.wait_ge(small_done, 1)
                for j in range(4):
                    s, a = j % 2, j // 2
                    h = 4 * g + j
                    rows = slice(32 * j, 32 * j + 32)
                    p0 = prob[:, (sg * UNITS + 2 * gg + s) % P_RING, a * S:(a + 1) * S]
                    p1 = prob[:, (sg * UNITS + 4 + s) % P_RING, (2 * gg + a) * P:(2 * gg + a + 1) * P]
                    pe.matmul(ps[rows, PVB + g % 2, 0:S], v_aug[:, b % 2, 0, h, :], p0, start=True, stop=True)
                    mm = pe.matmul(ps[rows, PVB + g % 2, P:S], v_aug[:, b % 2, 1, h, :], p1,
                                   start=False, stop=True, skip_group_check=True)
                mm.then_inc(pv_done, 1)

            def outputs_t(b):
                pe.wait_ge(o_evac, 4 * (b + 1))
                for t in range(TB):
                    bank = claim(("O", b, t))
                    for g in range(4):
                        tr = pe.transpose(ps[:, bank, g * P:(g + 1) * P], o_t[:, g, t * P:(t + 1) * P], ident[:, :])
                    tr.then_inc(work_full, 1)

            stacks_t(0)
            row_scores(0)
            maxima_t(0)
            for b in range(B):
                scores_t(b, 0)
                if b + 1 < B:
                    stacks_t(b + 1)
                scores_t(b, 1)
                weigh(b, 0)
                weigh(b, 1)
                if b + 1 < B:
                    row_scores(b + 1)
                weigh(b, 2)
                if b + 1 < B:
                    maxima_t(b + 1)
                weigh(b, 3)
                outputs_t(b)

            pe.wait_ge(exp_done, 2 * B * UNITS)
            for j in range(4):
                tg, k = j // 2, j % 2
                pe.wait_ge(y_ready, 4 * (tg + 1))
                for a in range(4):
                    tr = pe.transpose(ps[:, j, a * P:(a + 1) * P], y[:, 4 * tg + a, k * P:(k + 1) * P], ident[:, :])
                tr.then_inc(yt_full, 1)
            pe.wait_ge(work_dve, work_dve_total)
            for i in range(NT):
                pe.wait_ge(ylo_ready, 2 * (i // 4) + 2)
                for k in range(KD):
                    for half in (y_hi, y_lo):
                        mm = pe.matmul(ps[:, WORK, i * 2 * E:(i + 1) * 2 * E], half[:, k, i * P:(i + 1) * P],
                                       wr_t[:, k, :], start=(k == 0 and half is y_hi),
                                       stop=(k == KD - 1 and half is y_lo))
            mm.then_inc(lg_full, 1)

            def gate_up(e, par, c, first=False):
                n = CH * e + c
                tg, f = c // FD, c % FD
                b0 = 2 * (c % 2)
                fwait(pe, u_ready, n - 1)
                if c == 0:
                    pe.wait_ge(w_hi, 2 * e + 1)
                    pe.wait_ge(w_lo, 3 * e + 2)
                tok = slice(tg * GRP, (tg + 1) * GRP)
                for g in range(2):
                    for k in range(KD):
                        hi = gu_hi[:, par, k, g, f * P:(f + 1) * P]
                        lo = gu_lo[:, par, k, g, f * P:(f + 1) * P]
                        o = ps[:, b0 + g, :]
                        pe.matmul(o, hi, y_hi[:, k, tok], start=(k == 0), stop=False)
                        pe.matmul(o, hi, y_lo[:, k, tok], start=False, stop=False)
                        mm = pe.matmul(o, lo, y_hi[:, k, tok], start=False, stop=(k == KD - 1))
                mm.then_inc(gu_done, 1)

            def down(n, e, par, c):
                tg, f = c // FD, c % FD
                pe.wait_ge(hlo_ready, n + 1)
                pe.wait_ge(hhi_ready, n + 1)
                pe.wait_ge(w_lo, 3 * e + 3)
                for m in range(KD):
                    hi = dn_hi[:, par, f, m * P:(m + 1) * P]
                    lo = dn_lo[:, par, f, m * P:(m + 1) * P]
                    o = ps[:, 4 + 2 * tg + m, :]
                    pe.matmul(o, hi, h_hi[:, c, :], start=False, stop=True, skip_group_check=True)
                    pe.matmul(o, hi, h_lo[:, c, :], start=False, stop=True, skip_group_check=True)
                    mm = pe.matmul(o, lo, h_hi[:, c, :], start=False, stop=True, skip_group_check=True)
                mm.then_inc(dn_done, 1)

            def expert(e, par, first):
                for c in range(CH):
                    n = CH * e + c
                    gate_up(e, par, c)
                    if first and c == 0:
                        pe.wait_ge(score_ready, 1)
                        pe.wait_ge(lg_copied, 1)
                        pe.wait_ge(o_evac, 4 * B)
                        for i in range(NT):
                            tr = pe.transpose(ps[0:E, 5 + i // 4, (i % 4) * P:(i % 4 + 1) * P], score[:, i, :],
                                              ident[:, :])
                            if i % 4 == 3:
                                tr.then_inc(score_tr, 1)
                    if first and c == 1:
                        pe.wait_ge(score_t_ready, 2)
                        for tg in range(NG):
                            for m in range(KD):
                                pe.matmul(ps[:, 4 + 2 * tg + m, :], bdn_sb[:, m * P:(m + 1) * P],
                                          score_t[:, tg * GRP:(tg + 1) * GRP], start=True, stop=True,
                                          skip_group_check=True)
                    if c >= 2:
                        down(n - 2, e, par, c - 2)
                    elif not first:
                        down(n - 2, e - 1, 1 - par, c + 2)

            expert(0, 0, True)
            expert(1, 1, False)
            with pe.Fori(1, E // 2) as i:
                expert(2 * i, 0, False)
                expert(2 * i + 1, 1, False)
            down(CH * E - 2, E - 1, 1, 2)
            down(CH * E - 1, E - 1, 1, 3)

            for j in range(4):
                tg = j // 2
                pe.wait_ge(outt_ready[0], tg + 1)
                pe.wait_ge(outt_ready[1], tg + 1)
                for a in range(2):
                    for m in range(KD):
                        col = ((2 * j + a) % 4) * P
                        tr = pe.transpose(ps[:, j, (a * KD + m) * P:(a * KD + m + 1) * P],
                                          out_t[:, tg, m, col:col + P], ident[:, :])
                tr.then_inc(out_tr, 1)


_INS = ['x', 'ctx_2048', 'L0_ffn_router_weight', 'L0_ffn_router_bias', 'L0_ffn_gate_up_proj',
        'L0_ffn_gate_up_proj_bias', 'L0_ffn_down_proj', 'L0_ffn_down_proj_bias']


def kernel(**inputs):
    import numpy as _np
    import concourse.bacc as _bacc
    from concourse import mybir as _mybir
    from concourse.bass_utils import run_bass_kernel_spmd as _run

    nc = _bacc.Bacc("TRN2", target_bir_lowering=False, num_devices=1)
    arrays, args = {}, []
    for name in _INS:
        a = _np.ascontiguousarray(inputs[name])
        arrays[f"in_{name}_dram"] = a
        args.append(nc.dram_tensor(f"in_{name}_dram", a.shape, _mybir.dt.from_np(a.dtype), kind="ExternalInput").ap())
    tokens = args[0].shape[0] * args[0].shape[1]
    scores = nc.dram_tensor("scores_dram", (args[2].shape[0], tokens), _mybir.dt.float32, kind="Internal").ap()
    out = nc.dram_tensor("out_0_dram", args[0].shape, _mybir.dt.float32, kind="ExternalOutput").ap()
    xattn_moe(nc, *args, scores, out)
    r = _run(nc, [arrays], core_ids=[0])
    return r.results[0]["out_0_dram"]
```

```python
import math
from contextlib import ExitStack

import concourse.bass as bass
from concourse import mybir

F32 = mybir.dt.float32
F32R = mybir.dt.float32r
BF16 = mybir.dt.bfloat16
U32 = mybir.dt.uint32
ALU = mybir.AluOpType
ACT = mybir.ActivationFunctionType
AX = mybir.AxisListType

P = 128
NEG = -1.0e30
EPS = 1e-5
ALPHA = 1.702
LIMIT = 7.0
TOP_K = 4


def xattn_moe(nc, x, ctx_in, w_router, b_router, w_gu, b_gu, w_dn, b_dn, score_dram, out):
    B, S, D = x.shape
    E = w_router.shape[0]
    H = 16
    HD = D // H
    PAIRS = H // 2
    T = B * S
    NT = T // P
    TB = S // P
    KD = D // P
    F = w_dn.shape[1]
    FD = F // P
    SC = 1.0 / HD ** 0.5
    ST = 64
    GRP = 512
    NG = T // GRP
    CH = NG * FD
    UNITS = 6
    ST_RING, P_RING = 4, 12
    assert (B, TB, KD, FD, NG) == (4, 2, 2, 2, 2)

    with ExitStack() as es:
        def sb(name, shape, dt=F32):
            return es.enter_context(nc.sbuf_tensor(name, shape, dt))

        def sem(name):
            return es.enter_context(nc.semaphore(name))

        ps = es.enter_context(nc.psum_tensor("ps", [P, 8, 512], F32))
        SCORE, WORK, PVB = (0, 1, 2, 3), (4, 5, 6), 7

        ident = sb("ident", [P, P])
        ident_b = sb("ident_b", [P, P], BF16)
        mask_diag = sb("mask_diag", [P, 4, P], BF16)
        iota_e = sb("iota_e", [P, E])
        neg_half = sb("neg_half", [P, TB])

        euler = sb("euler", [P, NT // 2, TOP_K])
        sel_f = sb("sel_f", [P, 2, P])
        sel = sb("sel", [P, 2, P], F32R)

        x_tok = sb("x_tok", [P, NT, D])
        ctx_tok = sb("ctx_tok", [P, NT, D])
        stats = sb("stats", [P, NT, 6])
        mv = sb("mv", [P, NT, 2])
        var_eps = sb("var_eps", [P, 2, NT])
        rstd = sb("rstd", [P, 2, NT])
        shift = sb("shift", [P, 2, NT])
        q_norm = sb("q_norm", [P, 2, TB, D])
        q_stack = sb("q_stack", [P, 2, TB, H, ST], F32R)
        k_stack = sb("k_stack", [P, 2, TB, H, ST], F32R)
        q_t = sb("q_t", [P, 2, PAIRS, S], F32R)
        k_t = sb("k_t", [P, 2, PAIRS, 2, S], F32R)
        v_aug = sb("v_aug", [P, 2, TB, H, 32])
        neg_max = sb("neg_max", [P, 2, TB, 2, PAIRS])
        max_t = sb("max_t", [H, 2, S], F32R)
        prob = sb("prob", [P, P_RING, 512])
        o_t = sb("o_t", [P, 4, S])
        r_den = sb("r_den", [P, TB, H])
        attn = sb("attn", [P, TB, D])

        y = ctx_tok
        y_hi = k_t[:, 0, 0:4, :, :].rearrange("p (k a) h s -> p k (a h s)", k=KD)
        y_lo = k_t[:, 0, 4:8, :, :].rearrange("p (k a) h s -> p k (a h s)", k=KD)
        wr_sb = sb("wr_sb", [E, D])
        br_sb = sb("br_sb", [P, E])
        wr_t = sb("wr_t", [P, KD, 2 * E], F32R)
        bgu_sb = sb("bgu_sb", [E, 2 * F])
        bias_g = sb("bias_g", [P, FD, E])
        bias_u = sb("bias_u", [P, FD, E])
        bdn_raw = sb("bdn_raw", [3 * E, D])
        bdn_tmp = sb("bdn_tmp", [3 * E, D], F32R)
        bdn_st = sb("bdn_st", [P, D], F32R)
        lg2 = sb("lg2", [P, NT, 2 * E])
        logits = sb("logits", [P, NT, E])
        top8 = sb("top8", [P, NT, 8])
        idx8 = sb("idx8", [P, NT, 8], U32)
        idx_f = sb("idx_f", [P, NT, TOP_K])
        top_d = sb("top_d", [P, NT, TOP_K])
        top_e = sb("top_e", [P, NT, TOP_K])
        top_s = sb("top_s", [P, NT])
        top_r = sb("top_r", [P, NT])
        top_w = sb("top_w", [P, NT, TOP_K])
        onehot = sb("onehot", [P, NT * TOP_K, E])
        onehot_w = sb("onehot_w", [P, NT * TOP_K, E])
        score_st = sb("score_st", [P, NT, P], F32R)
        score_sT = sb("score_sT", [P, T], F32R)
        score_t = sb("score_t", [64 + E, T])
        score_b = q_stack[:, 0, :, :, :].bitcast(F32).rearrange("p t h c -> p t (h c)")

        raw_gu = sb("raw_gu", [P, 2, KD, 2 * F])
        raw_dn = sb("raw_dn", [P, 2, FD, D])
        out_t = raw_gu
        out_sb = ctx_tok
        gu_hi = sb("gu_hi", [P, 2, KD, 2, F], F32R)
        gu_lo = sb("gu_lo", [P, 2, KD, 2, F], F32R)
        dn_hi = sb("dn_hi", [P, 2, FD, D], F32R)
        dn_lo = sb("dn_lo", [P, 2, FD, D], F32R)
        hid, gate, sig = prob[:, 0:4, :], prob[:, 4:6, :], prob[:, 6:8, :]
        glu, up = prob[:, 8:10, :], prob[:, 10:12, :]
        up_s = q_norm.rearrange("p a t d -> p a (t d)")
        h_hi = q_t[:, 0, :, :].rearrange("p (c a) s -> p c (a s)", c=CH)
        h_lo = q_t[:, 1, :, :].rearrange("p (c a) s -> p c (a s)", c=CH)

        x_in = [sem(f"x_in{b}") for b in range(B)]
        ctx_dma = [sem(f"ctx_in{b}") for b in range(B)]
        small_in = sem("small_in")
        v_pads = sem("v_pads")
        small_pads = sem("small_pads")
        consts = sem("consts")
        pool_step = sem("pool_step")
        dve_step = sem("dve_step")
        var_ready = sem("var_ready")
        rstd_ready = sem("rstd_ready")
        k_pads0 = sem("k_pads0")
        k_pads = sem("k_pads")
        small_t = sem("small_t")
        small_done = sem("small_done")
        q_norm_ready = sem("q_norm_ready")
        stack_hi = sem("stack_hi")
        stack_dup = sem("stack_dup")
        stack_lo = sem("stack_lo")
        v_ready = sem("v_ready")
        work_full = sem("work_full")
        work_act = sem("work_act")
        work_dve = sem("work_dve")
        max_rows = [sem("max_rows0"), sem("max_rows1")]
        st_full = sem("st_full")
        exp_done = sem("exp_done")
        sel_done = sem("sel_done")
        pv_done = sem("pv_done")
        o_evac = sem("o_evac")
        y_ready = sem("y_ready")
        topd_ready = sem("topd_ready")
        tope_ready = sem("tope_ready")
        score_ready = sem("score_ready")
        score_t_ready = sem("score_t_ready")
        score_out = sem("score_out")
        yhi_ready = sem("yhi_ready")
        ylo_ready = sem("ylo_ready")
        score_in = [[sem(f"score_in{p}{g}") for g in range(NG)] for p in range(2)]
        sel_full = sem("sel_full")
        score_sel = sem("score_sel")
        raw_in = [sem("raw_in0"), sem("raw_in1")]
        w_hi = sem("w_hi")
        w_lo = sem("w_lo")
        gu_done = sem("gu_done")
        g_ready = sem("g_ready")
        u_ready = sem("u_ready")
        us_ready = sem("us_ready")
        sig_ready = sem("sig_ready")
        glu_ready = sem("glu_ready")
        h_ready = sem("h_ready")
        hhi_ready = sem("hhi_ready")
        hlo_ready = sem("hlo_ready")
        dn_done = sem("dn_done")
        outt_ready = [sem("outt_act"), sem("outt_dve")]
        out_tr = sem("out_tr")
        out_ready = sem("out_ready")
        out_dma = sem("out_dma")

        def fwait(eng, s, n):
            if not isinstance(n, int) or n > 0:
                eng.wait_ge(s, n)

        def slot(b):
            def of(kind, batch, numbers):
                return [(kind, batch, n) for n in numbers]

            old = b - 1
            if b + 1 < B:
                new = b + 1
                order = [("T", new, (0, 1, 2)), ("V", old, (4,)), ("T", new, (3,)), ("S", b, (0,)), ("V", old, (5,)),
                         ("T", new, (4, 5)), ("V", old, (6,)), ("T", new, (6,)), ("S", b, (1,)), ("V", old, (7,)),
                         ("T", new, (7,)), ("X", new, (0, 1)), ("O", old, (0,)), ("X", new, (2,)), ("O", old, (1,)),
                         ("S", b, (2,)), ("X", new, (3, 4)), ("V", b, (0,)), ("X", new, (5, 6)), ("S", b, (3,)),
                         ("V", b, (1,)), ("X", new, (7, 8, 9)), ("S", b, (4,)), ("V", b, (2,)), ("X", new, (10, 11)),
                         ("S", b, (5,)), ("V", b, (3,)), ("M", new, (0,))]
            else:
                order = [("V", old, (4, 5)), ("S", b, (0,)), ("Y", 0, (0,)), ("Y", 1, (0,)), ("V", old, (6,)),
                         ("L", 0, (0,)), ("V", old, (7,)), ("S", b, (1,)), ("O", old, (0, 1)), ("S", b, (2,)),
                         ("V", b, (0, 1)), ("S", b, (3,)), ("V", b, (2, 3)), ("R", 0, (0,)), ("S", b, (4, 5)),
                         ("Y", 2, (0,)), ("V", b, (4, 5, 6, 7)), ("O", b, (0, 1))]
            return [u for kind, batch, numbers in order if batch >= 0 for u in of(kind, batch, numbers)]

        steps = [("T", 0, n) for n in range(8)] + [("X", 0, n) for n in range(12)] + [("M", 0, 0)]
        for b in range(B):
            steps += slot(b)
        late = [("Y", B - 1, 0), ("L", 1, 0), ("R", 1, 0)]
        PARTS = [(0, NT // 2), (NT // 2, NT)]

        def t_use(n):
            return n // 4, (n // 2) % 2, n % 2

        def x_use(n):
            if n < 4:
                return 0, n // 2, 4 * (n % 2), 4, P
            n -= 4
            return 1, n // 4, 2 * (n % 4), 2, S

        def st_unit(i):
            if i < 4:
                return i % 2, 2 * (i // 2), 2, 0, 0
            return i % 2, 0, 4, 1, P

        uses = [u for u in steps + late if u[0] in "TXMOYLR"]
        slot_of = {u: i for i, u in enumerate(uses)}
        emptied = []
        n_act = n_dve = 0
        for kind, _, n in uses:
            if kind == "T" and t_use(n)[2] == 1:
                n_act += 2
                emptied.append((work_act, n_act))
            else:
                n_dve += 1
                emptied.append((work_dve, n_dve))
        bank_of, before = [], []
        last_use = {}
        for i, (kind, b, _) in enumerate(uses):
            free = WORK if i < len(uses) - len(late) else WORK[:2]
            if b == 0 and kind in "TX":
                free = WORK + SCORE
            bank = min(free, key=lambda k: last_use.get(k, -1))
            bank_of.append(bank)
            before.append(last_use.get(bank))
            last_use[bank] = i
            if uses[i] == ("X", 0, 11):
                first_batch = dict(last_use)
            if i == len(uses) - len(late) - 1:
                attention_last = dict(last_use)

        def work_bank(use):
            return bank_of[slot_of[use]]

        def acc_bank(tg, m):
            return (6, 4)[tg] + m

        block = es.enter_context(nc.Block())

        @block.sync
        def _(sp):
            def load_weights(e, par):
                sp.dma_start(raw_gu[:, par, :, :], w_gu[e].rearrange("(k p) n -> p k n", p=P)
                             ).then_inc(raw_in[par], 16)
                sp.dma_start(raw_dn[:, par, :, :], w_dn[e].rearrange("(k p) n -> p k n", p=P)
                             ).then_inc(raw_in[par], 16)

            def load_scores(e, par, tg):
                sp.dma_start(score_b[:, par, tg * GRP:(tg + 1) * GRP],
                             score_dram[e, tg * GRP:(tg + 1) * GRP].partition_broadcast(P)
                             ).then_inc(score_in[par][tg], 16)

            for b in range(B):
                sp.dma_start(x_tok[:, TB * b:TB * b + TB, :], x[b].rearrange("(t p) d -> p t d", p=P)
                             ).then_inc(x_in[b], 16)
                if b >= 1:
                    sp.dma_start(ctx_tok[:, TB * b:TB * b + TB, :], ctx_in[b].rearrange("(t p) d -> p t d", p=P)
                                 ).then_inc(ctx_dma[b], 16)
            sp.dma_start(wr_sb[:, :], w_router[:, :]).then_inc(small_in, 16)
            sp.dma_start(bgu_sb[:, :], b_gu[:, :]).then_inc(small_in, 16)
            sp.dma_start(br_sb[:, :], b_router.partition_broadcast(P)).then_inc(small_in, 16)
            for j in range(3):
                sp.dma_start(bdn_raw[j * E:(j + 1) * E, :], b_dn[:, :]).then_inc(small_in, 16)
            load_weights(0, 0)
            load_weights(1, 1)
            for b in range(B):
                sp.wait_ge(*emptied[slot_of[("M", b, 0)]])
                for s in range(2):
                    sp.dma_start(q_t[64 * s + 32:64 * s + 33, b % 2, :, :].bitcast(F32),
                                 max_t[PAIRS * s:PAIRS * (s + 1), b % 2, :].bitcast(F32)
                                 ).then_inc(max_rows[b % 2], 16)
            for part in range(2):
                lo, hi = PARTS[part]
                sp.wait_ge(score_t_ready, part + 1)
                sp.dma_start(score_dram[:, lo * P:hi * P], score_t[64:64 + E, lo * P:hi * P]
                             ).then_inc(score_out, 16)
                sp.wait_ge(score_out, 16 * (part + 1))
                if part == 0:
                    for par in range(2):
                        load_scores(par, par, 0)
            with sp.Fori(0, E // 2 - 1) as i:
                for par in range(2):
                    e = 2 * i + par
                    sp.wait_ge(w_hi, 2 * e + 2)
                    sp.wait_ge(w_lo, 3 * e + 3)
                    load_weights(e + 2, par)
                    for tg in range(NG):
                        sp.wait_ge(us_ready, CH * e + FD * (tg + 1))
                        load_scores(e + 2, par, tg)
            for j in range(4):
                sp.wait_ge(out_ready, j + 1)
                sp.dma_start(out[j].rearrange("(t p) d -> p t d", p=P), out_sb[:, 2 * j:2 * j + 2, :]
                             ).then_inc(out_dma, 16)
            sp.wait_ge(out_dma, 64)

        @block.gpsimd
        def _(pool):
            done = [0]

            def step(ins):
                done[0] += 1
                ins.then_inc(pool_step, 1)

            def settle():
                pool.wait_ge(pool_step, done[0])

            step(pool.memset(ident[:, :], 0.0))
            settle()
            pool.affine_select(out=ident[:, :], in_=ident[:, :], compare_op=ALU.not_equal, fill=1.0, base=0,
                               pattern=[[-1, P]], channel_multiplier=1).then_inc(consts, 1)
            step(pool.memset(neg_half[:, :], -0.5))
            step(pool.memset(euler[:, :, :], math.e))

            def rsqrt(b, which):
                pool.wait_ge(var_ready, B * which + b + 1)
                t = slice(TB * b, TB * b + TB)
                pool.tensor_tensor(rstd[:, which, t], var_eps[:, which, t], neg_half[:, :], ALU.pow
                                   ).then_inc(rstd_ready, 1)

            def stack_pads(par):
                for t in range(TB):
                    pool.memset(q_stack[:, par, t, :, 32:48].bitcast(F32), 0.0).then_inc(consts, 1)
                    pool.memset(k_stack[:, par, t, :, 32:48].bitcast(F32), 0.0).then_inc(consts, 1)
                pool.wait_ge(consts, 1 + 6 * par + 4)
                for t in range(TB):
                    pool.memset(k_stack[:, par, t, :, 32:33].bitcast(F32), 1.0).then_inc(consts, 1)

            def dup(b):
                par = b % 2
                pool.wait_ge(stack_hi, 2 * b + 2)
                qs = q_stack[:, par, :, :, :].rearrange("p t h c -> p (t h) c")
                ks = k_stack[:, par, :, :, :].rearrange("p t h c -> p (t h) c")
                pool.tensor_scalar(qs[:, :, 48:64], qs[:, :, 0:16].bitcast(F32), 1.0, 1.0, ALU.mult, ALU.mult
                                   ).then_inc(stack_dup, 1)
                pool.tensor_scalar(ks[:, :, 16:32], ks[:, :, 0:16].bitcast(F32), 1.0, 1.0, ALU.mult, ALU.mult
                                   ).then_inc(stack_dup, 1)

            def values(b):
                pool.wait_ge(ctx_dma[b], 16)
                if b >= 2:
                    pool.wait_ge(pv_done, 2 * (b - 1))
                for t in range(TB):
                    pool.tensor_scalar(v_aug[:, b % 2, t, :, 0:HD],
                                       ctx_tok[:, TB * b + t, :].rearrange("p (h d) -> p h d", h=H),
                                       1.0, 1.0, ALU.mult, ALU.mult).then_inc(v_ready, 1)

            def select(u):
                pool.wait_ge(exp_done, u + 1)
                w, n = (S, 2) if u % UNITS < 4 else (P, 4)
                blk = prob[:, u % P_RING, :].rearrange("p (h q) -> p h q", q=w)[:, :, 0:P]
                pool.affine_select(out=blk, in_=blk, compare_op=ALU.is_ge, fill=0.0, base=0,
                                   pattern=[[0, n], [1, P]], channel_multiplier=-1).then_inc(sel_done, 1)

            def top_exp(part):
                lo, hi = PARTS[part]
                pool.wait_ge(topd_ready, part + 1)
                pool.tensor_tensor(top_e[:, lo:hi, :], euler[:, :, :], top_d[:, lo:hi, :], ALU.pow
                                   ).then_inc(tope_ready, 1)

            def lo_gu(e, par, k):
                pool.wait_ge(w_hi, 2 * e + 1)
                pool.tensor_tensor(gu_lo[:, par, k, :, :],
                                   raw_gu[:, par, k, :].rearrange("p (d g) -> p g d", g=2),
                                   gu_hi[:, par, k, :, :].bitcast(F32), ALU.subtract).then_inc(w_lo, 1)

            def lo_dn(e, par):
                pool.wait_ge(w_hi, 2 * e + 2)
                pool.tensor_tensor(dn_lo[:, par, :, :], raw_dn[:, par, :, :],
                                   dn_hi[:, par, :, :].bitcast(F32), ALU.subtract).then_inc(w_lo, 1)

            def key_pads(par, v):
                rows = slice(64 - 64 * v, 128 - 64 * v)
                pool.memset(k_t[rows, par, :, v, :].bitcast(F32), 0.0).then_inc(k_pads, 1)

            stack_pads(0)
            settle()
            rsqrt(0, 0)
            dup(0)
            pool.wait_ge(stack_dup, 2)
            key_pads(0, 1)
            pool.wait_ge(k_pads, 1)
            step(pool.memset(ident_b[:, :], 0.0))
            step(pool.memset(mask_diag[:, :, :], 0.0))
            settle()
            pool.affine_select(out=ident_b[:, :], in_=ident_b[:, :], compare_op=ALU.not_equal, fill=1.0, base=0,
                               pattern=[[-1, P]], channel_multiplier=1).then_inc(consts, 1)
            pool.affine_select(out=mask_diag[:, :, :], in_=mask_diag[:, :, :], compare_op=ALU.is_ge, fill=NEG,
                               base=0, pattern=[[0, 4], [-1, P]], channel_multiplier=1).then_inc(consts, 1)
            for b in range(1, B):
                rsqrt(b, 0)
            pool.memset(v_aug[:, :, :, :, HD:32].rearrange("p a t h c -> p (a t h) c"), 0.0).then_inc(v_pads, 1)
            pool.wait_ge(v_pads, 1)
            pool.memset(v_aug[:, :, :, :, HD:HD + 1].rearrange("p a t h c -> p (a t h) c"), 1.0
                        ).then_inc(v_pads, 1)
            values(0)
            for par in (1,):
                for t in range(TB):
                    pool.memset(q_stack[:, par, t, :, 32:48].bitcast(F32), 0.0).then_inc(consts, 1)
                    pool.memset(k_stack[:, par, t, :, 32:48].bitcast(F32), 0.0).then_inc(consts, 1)
                pool.wait_ge(consts, 13)
                for t in range(TB):
                    pool.memset(k_stack[:, par, t, :, 32:33].bitcast(F32), 1.0).then_inc(consts, 1)
            pool.wait_ge(consts, 15)
            for v in range(2):
                key_pads(1, v)
                pool.wait_ge(k_pads, v + 2)
            dup(1)
            pool.iota(iota_e[:, :], pattern=[[1, E]], base=0, channel_multiplier=0,
                      allow_small_or_imprecise_dtypes=True).then_inc(consts, 1)
            step(pool.memset(sel_f[:, :, :], 0.0))
            for row in (0, E):
                settle()
                step(pool.affine_select(out=sel_f[:, :, :], in_=sel_f[:, :, :], compare_op=ALU.not_equal, fill=1.0,
                                        base=-row, pattern=[[-1, 2], [0, P]], channel_multiplier=1))
            settle()
            pool.tensor_scalar(sel[:, :, :], sel_f[:, :, :], 1.0, 1.0, ALU.mult, ALU.mult).then_inc(consts, 1)
            values(1)
            pool.memset(bdn_st[:, :].bitcast(F32), 0.0).then_inc(small_pads, 1)
            pool.memset(score_st[:, :, :].bitcast(F32), 0.0).then_inc(small_pads, 1)
            for kind, b, n in steps:
                if kind == "S":
                    u = 2 * UNITS * b + 2 * n
                    select(u)
                    select(u + 1)
                    if n == 2:
                        if 2 <= b + 1 < B:
                            values(b + 1)
                        if b >= 1:
                            rsqrt(b - 1, 1)
                    if n in (4, 5) and b == 1:
                        lo_gu(0, 0, n - 4)
                    if n == 3 and b + 2 < B:
                        dup(b + 2)
                    if n == 3 and b == 2:
                        lo_dn(0, 0)
                    if n == 1 and b == B - 1:
                        top_exp(0)
            rsqrt(B - 1, 1)

            def expert(e, par, first, last):
                for c in range(CH):
                    n = CH * e + c
                    pool.wait_ge(sig_ready, n + 1)
                    fwait(pool, h_ready, n - 1)
                    pool.tensor_tensor(glu[:, c % 2, :], gate[:, c % 2, :], sig[:, c % 2, :],
                                       ALU.mult).then_inc(glu_ready, 1)
                    if not last and c < 2:
                        lo_gu(e + 1, 1 - par, c)
                    if not last and c == 2:
                        lo_dn(e + 1, 1 - par)
                    if first and c == 1:
                        top_exp(1)

            expert(0, 0, True, False)
            expert(1, 1, False, False)
            with pool.Fori(1, E // 2 - 1) as i:
                expert(2 * i, 0, False, False)
                expert(2 * i + 1, 1, False, False)
            expert(E - 2, 0, False, False)
            expert(E - 1, 1, False, True)

        @block.scalar
        def _(act):
            act.dma_start(ctx_tok[:, 0:TB, :], ctx_in[0].rearrange("(t p) d -> p t d", p=P)
                          ).then_inc(ctx_dma[0], 16)

            def stack_high(b):
                par = b % 2
                if b >= 2:
                    act.wait_ge(work_full, slot_of[("T", b - 2, 7)] + 1)
                act.wait_ge(ctx_dma[b], 16)
                qs = q_stack[:, par, :, :, :].rearrange("p t h c -> p (t h) c")
                ks = k_stack[:, par, :, :, :].rearrange("p t h c -> p (t h) c")
                act.activation(ks[:, :, 0:16], ctx_tok[:, TB * b:TB * b + TB, :]
                               .rearrange("p t (h d) -> p (t h) d", h=H), ACT.Copy).then_inc(stack_hi, 1)
                act.wait_ge(q_norm_ready, TB * (b + 1))
                act.activation(qs[:, :, 0:16], q_norm[:, par, :, :]
                               .rearrange("p t (h d) -> p (t h) d", h=H), ACT.Copy).then_inc(stack_hi, 1)

            def keys_out(b, n):
                t, half, _ = t_use(n)
                u = ("T", b, n)
                act.wait_ge(work_full, slot_of[u] + 1)
                if b >= 2:
                    act.wait_ge(st_full, 2 * UNITS * (b - 1))
                src = ps[:, work_bank(u), :].rearrange("p (a q) -> p a q", a=4)
                for v in range(2):
                    rows = slice(64 * v, 64 * v + 64)
                    act.activation(k_t[rows, b % 2, 4 * half:4 * half + 4, v, t * P:(t + 1) * P], src[rows],
                                   ACT.Copy).then_inc(work_act, 1)

            def exp_unit(u):
                act.wait_ge(st_full, u + 1)
                if u >= P_RING:
                    act.wait_ge(pv_done, u // UNITS - 1)
                act.activation(prob[:, u % P_RING, :], ps[:, u % ST_RING, :], ACT.Exp,
                               scale=SC).then_inc(exp_done, 1)

            def output_t(b, s2):
                act.wait_ge(pv_done, 2 * b + s2 + 1)
                if b >= 1:
                    act.wait_ge(work_full, slot_of[("O", b - 1, TB - 1)] + 1)
                act.activation(o_t[:, 2 * s2:2 * s2 + 2, :], ps[:, PVB, :].rearrange("p (g q) -> p g q", g=2),
                               ACT.Copy).then_inc(o_evac, 1)

            def tokens_high(b):
                act.wait_ge(work_full, slot_of[("Y", b, 0)] + 1)
                act.activation(y_hi[:, :, b * S:(b + 1) * S],
                               ps[:, work_bank(("Y", b, 0)), :].rearrange("p (k s) -> p k s", k=KD), ACT.Copy
                               ).then_inc(yhi_ready, 1)

            def split_gu(e, par):
                act.activation(gu_hi[:, par, :, :, :], raw_gu[:, par, :, :].rearrange("p k (d g) -> p k g d", g=2),
                               ACT.Copy).then_inc(w_hi, 1)

            def split_dn(e, par):
                act.activation(dn_hi[:, par, :, :], raw_dn[:, par, :, :], ACT.Copy).then_inc(w_hi, 1)

            stack_high(0)
            for kind, b, n in steps:
                if kind == "T" and t_use(n)[2] == 1:
                    keys_out(b, n)
                    if b == 0 and n == 7:
                        stack_high(1)
                elif kind == "S":
                    exp_unit(2 * UNITS * b + 2 * n)
                    exp_unit(2 * UNITS * b + 2 * n + 1)
                    if n == 3 and b == 1:
                        act.wait_ge(raw_in[0], 32)
                        split_gu(0, 0)
                    if n == 4 and b == 1:
                        split_dn(0, 0)
                    if n == 3 and b + 2 < B:
                        stack_high(b + 2)
                elif kind == "V" and n % 4 == 3:
                    output_t(b, n // 4)
                elif kind == "Y":
                    tokens_high(b)

            def high_half(n, c):
                act.wait_ge(h_ready, n + 1)
                fwait(act, dn_done, n - 3)
                act.activation(h_hi[:, c, :], hid[:, c, :], ACT.Copy).then_inc(hhi_ready, 1)

            def expert(e, par, first, last):
                for c in range(CH):
                    n = CH * e + c
                    if first and c == 3:
                        for j in range(2):
                            act.wait_ge(sel_full, j + 1)
                            act.activation(score_b[:, j, GRP:T], ps[:, acc_bank(1, j), :], ACT.Copy
                                           ).then_inc(score_sel, 1)
                    act.wait_ge(g_ready, n + 1)
                    fwait(act, glu_ready, n - 1)
                    act.activation(sig[:, c % 2, :], gate[:, c % 2, :], ACT.Sigmoid, scale=ALPHA
                                   ).then_inc(sig_ready, 1)
                    if first and c == 0:
                        tokens_high(B - 1)
                    else:
                        high_half(n - 1, (c - 1) % CH)
                    if not last and c == 0:
                        act.wait_ge(raw_in[1 - par], 16 * (e + par) + 32)
                        if not first:
                            act.wait_ge(gu_done, CH * e)
                        split_gu(e + 1, 1 - par)
                    if not last and c == 2:
                        if not first:
                            act.wait_ge(dn_done, CH * e)
                        split_dn(e + 1, 1 - par)

            expert(0, 0, True, False)
            expert(1, 1, False, False)
            with act.Fori(1, E // 2 - 1) as i:
                expert(2 * i, 0, False, False)
                expert(2 * i + 1, 1, False, False)
            expert(E - 2, 0, False, False)
            expert(E - 1, 1, False, True)
            high_half(CH * E - 1, CH - 1)
            for tg in range(NG):
                act.wait_ge(dn_done, CH * E - 2 * (NG - 1 - tg))
                act.activation(out_t[:, tg, 0, :], ps[:, acc_bank(tg, 0), :], ACT.Copy).then_inc(outt_ready[0], 1)

        @block.vector
        def _(dve):
            done = [0]

            def step(ins):
                done[0] += 1
                ins.then_inc(dve_step, 1)

            def settle():
                dve.wait_ge(dve_step, done[0])

            def row_stats(i):
                step(dve.bn_stats(stats[:, i, :], x_tok[:, i, :]))

            def variance(b, which):
                settle()
                for i in range(TB * b, TB * b + TB):
                    step(dve.bn_aggr(mv[:, i, :], stats[:, i, :]))
                settle()
                t = slice(TB * b, TB * b + TB)
                dve.tensor_scalar(var_eps[:, which, t], mv[:, t, 1], EPS, None, ALU.add).then_inc(var_ready, 1)

            def norm_shift(b, which):
                dve.wait_ge(rstd_ready, B * which + b + 1)
                t = slice(TB * b, TB * b + TB)
                step(dve.scalar_tensor_tensor(shift[:, which, t], mv[:, t, 0], -1.0, rstd[:, which, t],
                                              ALU.mult, ALU.mult))
                settle()

            def normalise(dst, i, which):
                return dve.tensor_scalar(dst, x_tok[:, i, :], rstd[:, which, i:i + 1], shift[:, which, i:i + 1],
                                         ALU.mult, ALU.add)

            def queries(b):
                norm_shift(b, 0)
                if b >= 2:
                    dve.wait_ge(stack_lo, 2 * b - 2)
                for t in range(TB):
                    normalise(q_norm[:, b % 2, t, :], TB * b + t, 0).then_inc(q_norm_ready, 1)

            def stack_low(b):
                par = b % 2
                dve.wait_ge(stack_hi, 2 * b + 2)
                dve.wait_ge(q_norm_ready, TB * (b + 1))
                src_q = q_norm[:, par, :, :].rearrange("p t (h d) -> p (t h) d", h=H)
                src_k = ctx_tok[:, TB * b:TB * b + TB, :].rearrange("p t (h d) -> p (t h) d", h=H)
                qs = q_stack[:, par, :, :, :].rearrange("p t h c -> p (t h) c")
                ks = k_stack[:, par, :, :, :].rearrange("p t h c -> p (t h) c")
                dve.tensor_tensor(ks[:, :, 48:64], src_k, ks[:, :, 0:16].bitcast(F32), ALU.subtract
                                  ).then_inc(stack_lo, 1)
                dve.tensor_tensor(qs[:, :, 16:32], src_q, qs[:, :, 0:16].bitcast(F32), ALU.subtract
                                  ).then_inc(stack_lo, 1)

            def queries_out(b, n):
                t, half, _ = t_use(n)
                u = ("T", b, n)
                dve.wait_ge(work_full, slot_of[u] + 1)
                if b >= 2:
                    dve.wait_ge(st_full, 2 * UNITS * (b - 1))
                dve.tensor_copy(q_t[:, b % 2, 4 * half:4 * half + 4, t * P:(t + 1) * P],
                                ps[:, work_bank(u), :].rearrange("p (a q) -> p a q", a=4)
                                ).then_inc(work_dve, 1)

            def row_max(b, n):
                t, s, p0, np_, keys = x_use(n)
                u = ("X", b, n)
                dve.wait_ge(work_full, slot_of[u] + 1)
                if b >= 2 and n == 0:
                    dve.wait_ge(work_full, slot_of[("M", b - 2, 0)] + 1)
                dve.tensor_reduce(neg_max[:, b % 2, t, s, p0:p0 + np_],
                                  ps[:, work_bank(u), :].rearrange("p (a k) -> p a k", k=keys),
                                  AX.X, ALU.max, negate=True).then_inc(work_dve, 1)

            def max_rows_t(b):
                u = ("M", b, 0)
                dve.wait_ge(work_full, slot_of[u] + 1)
                if b >= 2:
                    dve.wait_ge(max_rows[b % 2], 32 * (b // 2))
                dve.tensor_copy(max_t[:, b % 2, :], ps[0:H, work_bank(u), 0:S]).then_inc(work_dve, 1)

            def attn_out(b, t):
                u = ("O", b, t)
                i = TB * b + t
                dve.wait_ge(work_full, slot_of[u] + 1)
                settle()
                o = ps[:, work_bank(u), :].rearrange("p (h c) -> p h c", c=32)
                step(dve.reciprocal(r_den[:, t, :], o[:, :, HD]))
                settle()
                dve.tensor_tensor(attn[:, t, :].rearrange("p (h d) -> p h d", h=H), o[:, :, 0:HD],
                                  r_den[:, t, :].unsqueeze(2).to_broadcast([P, H, HD]), ALU.mult
                                  ).then_inc(work_dve, 1)
                dve.wait_ge(*emptied[slot_of[u]])
                step(dve.tensor_tensor(x_tok[:, i, :], x_tok[:, i, :], attn[:, t, :], ALU.add))
                settle()
                row_stats(i)

            def tokens(b):
                norm_shift(b, 1)
                dve.wait_ge(v_ready, TB * (b + 1))
                for t in range(TB):
                    normalise(y[:, TB * b + t, :], TB * b + t, 1).then_inc(y_ready, 1)

            def tokens_low(b):
                u = ("Y", b, 0)
                dve.wait_ge(yhi_ready, b + 1)
                cols = slice(b * S, (b + 1) * S)
                dve.tensor_tensor(y_lo[:, :, cols], ps[:, work_bank(u), :].rearrange("p (k s) -> p k s", k=KD),
                                  y_hi[:, :, cols].bitcast(F32), ALU.subtract).then_inc(work_dve, 1)

            def small_weights():
                dve.wait_ge(small_t, 1)
                wr_ps = ps[:, 7, 0:KD * E].rearrange("p (k e) -> p k e", k=KD)
                b_ps = ps[:, 7, KD * E:KD * E + 2 * FD * E].rearrange("p (g f e) -> p g f e", g=2, f=FD)
                step(dve.tensor_copy(wr_t[:, :, 0:E], wr_ps))
                step(dve.tensor_copy(bias_g[:, :, :], b_ps[:, 0, :, :]))
                step(dve.tensor_scalar(bias_u[:, :, :], b_ps[:, 1, :, :], 1.0, None, ALU.add))
                settle()
                dve.tensor_tensor(wr_t[:, :, E:2 * E], wr_ps, wr_t[:, :, 0:E].bitcast(F32), ALU.subtract
                                  ).then_inc(small_done, 1)

            def router(part):
                lo, hi = PARTS[part]
                m = hi - lo
                t = slice(lo, hi)
                u = ("L", part, 0)
                dve.wait_ge(work_full, slot_of[u] + 1)
                dve.tensor_copy(lg2[:, t, :], ps[:, work_bank(u), 0:m * 2 * E].rearrange("p (t c) -> p t c", t=m)
                                ).then_inc(work_dve, 1)
                dve.wait_ge(*emptied[slot_of[u]])
                step(dve.tensor_tensor(logits[:, t, :], lg2[:, t, 0:E], lg2[:, t, E:2 * E], ALU.add))
                settle()
                step(dve.tensor_tensor(logits[:, t, :], logits[:, t, :],
                                       br_sb[:, :].unsqueeze(1).to_broadcast([P, m, E]), ALU.add))
                settle()
                for i in range(lo, hi):
                    step(dve.max(top8[:, i, :], logits[:, i, :]))
                settle()
                dve.tensor_tensor(top_d[:, t, :], top8[:, t, 0:TOP_K], top8[:, t, 0:1].to_broadcast([P, m, TOP_K]),
                                  ALU.subtract).then_inc(topd_ready, 1)
                for i in range(lo, hi):
                    step(dve.max_index(idx8[:, i, :], top8[:, i, :], logits[:, i, :]))
                settle()
                step(dve.tensor_copy(idx_f[:, t, :], idx8[:, t, 0:TOP_K]))
                settle()
                tk = slice(lo * TOP_K, hi * TOP_K)
                step(dve.tensor_tensor(onehot[:, tk, :], iota_e[:, :].unsqueeze(1).to_broadcast([P, m * TOP_K, E]),
                                       idx_f[:, t, :].rearrange("p t k -> p (t k)").unsqueeze(2)
                                       .to_broadcast([P, m * TOP_K, E]), ALU.is_equal))
                dve.wait_ge(tope_ready, part + 1)
                step(dve.tensor_reduce(top_s[:, t], top_e[:, t, :], AX.X, ALU.add))
                settle()
                step(dve.reciprocal(top_r[:, t], top_s[:, t]))
                settle()
                step(dve.tensor_tensor(top_w[:, t, :], top_e[:, t, :],
                                       top_r[:, t].unsqueeze(2).to_broadcast([P, m, TOP_K]), ALU.mult))
                settle()
                step(dve.tensor_tensor(onehot_w[:, tk, :], onehot[:, tk, :],
                                       top_w[:, t, :].rearrange("p t k -> p (t k)").unsqueeze(2)
                                       .to_broadcast([P, m * TOP_K, E]), ALU.mult))
                settle()
                if part == 0:
                    dve.wait_ge(small_pads, 2)
                score = score_st[:, t, 64:64 + E].bitcast(F32)
                step(dve.tensor_reduce(score, onehot_w[:, tk, :].rearrange("p (t k) e -> p t e k", k=TOP_K),
                                       AX.X, ALU.add))
                settle()
                step(dve.tensor_copy(score_st[:, t, 0:E], score))
                step(dve.tensor_copy(score_st[:, t, 2 * E:3 * E], score))
                settle()
                dve.tensor_tensor(score_st[:, t, E:2 * E], score, score_st[:, t, 0:E].bitcast(F32), ALU.subtract
                                  ).then_inc(score_ready, 1)

            def scores_out(part, n):
                u = ("R", part, n)
                tiles = range(*PARTS[part])
                cols = slice(tiles[0] * P, (tiles[-1] + 1) * P)
                w = len(tiles) * P
                dve.wait_ge(work_full, slot_of[u] + 1)
                dve.tensor_copy(score_t[64:64 + E, cols], ps[64:64 + E, work_bank(u), 0:w]).then_inc(score_t_ready, 1)
                dve.tensor_copy(score_sT[:, cols], ps[:, work_bank(u), 0:w]).then_inc(work_dve, 1)

            dve.memset(k_t[P // 2:P, 0, :, 0, :].bitcast(F32), 0.0).then_inc(k_pads0, 1)
            dve.wait_ge(x_in[0], 16)
            row_stats(0)
            row_stats(1)
            variance(0, 0)
            for b in range(1, B):
                dve.wait_ge(x_in[b], 16)
                for t in range(TB):
                    row_stats(TB * b + t)
                if b == 1:
                    queries(0)
            stack_low(0)
            for b in range(1, B):
                variance(b, 0)
            for kind, b, n in steps:
                if kind == "T" and t_use(n)[2] == 0:
                    queries_out(b, n)
                    if b == 0 and n == 2:
                        queries(1)
                elif kind == "X":
                    row_max(b, n)
                elif kind == "M":
                    max_rows_t(b)
                    if b == 0:
                        stack_low(1)
                        small_weights()
                        dve.wait_ge(small_in, 96)
                        dve.wait_ge(small_pads, 1)
                        step(dve.tensor_copy(bdn_tmp[:, :], bdn_raw[:, :]))
                        step(dve.tensor_copy(bdn_st[0:2 * E, :], bdn_raw[0:2 * E, :]))
                        settle()
                        step(dve.tensor_tensor(bdn_st[2 * E:3 * E, :], bdn_raw[2 * E:3 * E, :],
                                               bdn_tmp[2 * E:3 * E, :].bitcast(F32), ALU.subtract))
                elif kind == "O":
                    attn_out(b, n)
                    if n == TB - 1:
                        variance(b, 1)
                elif kind == "S":
                    if n == 2 and b + 2 < B:
                        queries(b + 2)
                    if n == 4 and b + 2 < B:
                        stack_low(b + 2)
                    if n == 3 and b >= 1:
                        tokens(b - 1)
                elif kind == "Y":
                    tokens_low(b)
                elif kind == "L":
                    router(b)
                elif kind == "R":
                    scores_out(b, n)
            tokens(B - 1)

            def low_half(n, c):
                dve.wait_ge(hhi_ready, n + 1)
                fwait(dve, dn_done, n - 3)
                dve.tensor_tensor(h_lo[:, c, :], hid[:, c, :], h_hi[:, c, :].bitcast(F32), ALU.subtract
                                  ).then_inc(hlo_ready, 1)

            def hidden(n, c):
                dve.wait_ge(glu_ready, n + 1)
                dve.wait_ge(us_ready, n + 1)
                fwait(dve, hlo_ready, n - 3)
                dve.tensor_tensor(hid[:, c, :], up_s[:, c % 2, :], glu[:, c % 2, :], ALU.mult
                                  ).then_inc(h_ready, 1)

            def expert(e, par, first, second):
                for c in range(CH):
                    n = CH * e + c
                    tg, f = c // FD, c % FD
                    b0 = 2 * (c % 2)
                    dve.wait_ge(gu_done, n + 1)
                    fwait(dve, glu_ready, n - 1)
                    dve.tensor_scalar(gate[:, c % 2, :], ps[:, b0, :], bias_g[:, f, bass.ds(e, 1)], LIMIT,
                                      ALU.add, ALU.min).then_inc(g_ready, 1)
                    fwait(dve, us_ready, n - 1)
                    dve.tensor_scalar(up[:, c % 2, :], ps[:, b0 + 1, :], bias_u[:, f, bass.ds(e, 1)],
                                      LIMIT + 1.0, ALU.add, ALU.min).then_inc(u_ready, 1)
                    if first and c == 2:
                        scores_out(1, 0)
                    if not (first and c == 0):
                        hidden(n - 1, (c - 1) % CH)
                    dve.wait_ge(u_ready, n + 1)
                    fwait(dve, h_ready, n - 1)
                    if f == 0 and tg == 0:
                        dve.wait_ge(score_in[par][0], 8 * (e - par) + 16)
                    elif f == 0 and second:
                        dve.wait_ge(score_sel, e + 1)
                    elif f == 0:
                        dve.wait_ge(score_in[par][1], 8 * (e - par))
                    dve.scalar_tensor_tensor(up_s[:, c % 2, :], up[:, c % 2, :], 1.0 - LIMIT,
                                             score_b[:, par, tg * GRP:(tg + 1) * GRP], ALU.max, ALU.mult
                                             ).then_inc(us_ready, 1)
                    if not (first and c == 0):
                        low_half(n - 1, (c - 1) % CH)
                    if first and c == 0:
                        tokens_low(B - 1)
                    if first and c == 1:
                        router(1)

            expert(0, 0, True, True)
            expert(1, 1, False, True)
            with dve.Fori(1, E // 2) as i:
                expert(2 * i, 0, False, False)
                expert(2 * i + 1, 1, False, False)
            N = CH * E
            hidden(N - 1, CH - 1)
            low_half(N - 1, CH - 1)
            for tg in range(NG):
                dve.wait_ge(dn_done, N - 2 * (NG - 1 - tg))
                dve.tensor_copy(out_t[:, tg, 1, :], ps[:, acc_bank(tg, 1), :]).then_inc(outt_ready[1], 1)
            for j in range(4):
                dve.wait_ge(out_tr, j + 1)
                dve.tensor_tensor(out_sb[:, 2 * j:2 * j + 2, :], ps[:, j, :].rearrange("p (t d) -> p t d", t=2),
                                  x_tok[:, 2 * j:2 * j + 2, :], ALU.add).then_inc(out_ready, 1)

        @block.tensor
        def _(pe):
            def claim(use):
                i = slot_of[use]
                if before[i] is not None:
                    pe.wait_ge(*emptied[before[i]])
                return work_bank(use)

            def stacks_t(b, n):
                if n == 0:
                    pe.wait_ge(consts, (7, 15)[b % 2])
                    pe.wait_ge(stack_lo, 2 * b + 2)
                    pe.wait_ge(stack_dup, 2 * b + 2)
                t, half, which = t_use(n)
                bank = claim(("T", b, n))
                src = (q_stack, k_stack)[which]
                for j in range(4):
                    pair = 4 * half + j
                    tr = pe.transpose(ps[:, bank, j * P:(j + 1) * P],
                                      src[:, b % 2, t, 2 * pair:2 * pair + 2, :].bitcast(F32)
                                      .rearrange("p h c -> p (h c)"), ident[:, :])
                tr.then_inc(work_full, 1)

            def row_scores(b, n):
                t, s, p0, np_, keys = x_use(n)
                bank = claim(("X", b, n))
                if n in (0, 4):
                    for last in (4 * t + 2, 4 * t + 3):
                        pe.wait_ge(*emptied[slot_of[("T", b, last)]])
                if n == 0:
                    pe.wait_ge(k_pads0, 1)
                    pe.wait_ge(k_pads, 2 * min(b, 1) + 1)
                    pe.wait_ge(consts, 9)
                for j in range(np_):
                    pe.matmul(ps[:, bank, j * keys:(j + 1) * keys],
                              q_t[:, b % 2, p0 + j, t * P:(t + 1) * P],
                              k_t[:, b % 2, p0 + j, s, 0:keys], start=(j == 0), stop=True,
                              skip_group_check=True)
                diag = ps[:, bank, :].rearrange("p (a k) -> p a k", k=keys)[:, :, keys - P:keys]
                pe.matmul(diag, ident_b[:, :], mask_diag[:, 0:np_, :], start=False, stop=True,
                          skip_group_check=True).then_inc(work_full, 1)

            def maxima_t(b):
                bank = claim(("M", b, 0))
                pe.wait_ge(*emptied[slot_of[("X", b, 11)]])
                for t in range(TB):
                    tr = pe.transpose(ps[0:H, bank, t * P:(t + 1) * P],
                                      neg_max[:, b % 2, t, :, :].rearrange("p s a -> p (s a)"), ident[:, :])
                tr.then_inc(work_full, 1)

            def scores(b, n):
                if n == 0:
                    pe.wait_ge(max_rows[b % 2], 32 * (b // 2 + 1))
                u = 2 * UNITS * b + 2 * n
                s2, i = n // 3, 2 * (n % 3)
                fwait(pe, exp_done, u + 2 - ST_RING)
                for v in range(2):
                    if u < ST_RING:
                        pe.wait_ge(*emptied[first_batch[u + v]])
                    s, p0, np_, kt, q0 = st_unit(i + v)
                    w = S - q0
                    for j in range(np_):
                        pair = 4 * s2 + p0 + j
                        mm = pe.matmul(ps[:, (u + v) % ST_RING, j * w:(j + 1) * w],
                                       k_t[:, b % 2, pair, s, kt * P:(kt + 1) * P],
                                       q_t[:, b % 2, pair, q0:S], start=True, stop=True)
                    mm.then_inc(st_full, 1)

            def weigh(b, n):
                g, gg, s2 = n // 2, (n // 2) % 2, n // 4
                sg = 2 * b + s2
                col = (g % 2) * S
                pe.wait_ge(sel_done, UNITS * (sg + 1))
                pe.wait_ge(v_ready, TB * (b + 1))
                if b == 0 and n == 0:
                    pe.wait_ge(v_pads, 2)
                    pe.wait_ge(small_done, 1)
                if n % 4 == 0:
                    fwait(pe, o_evac, sg)
                for j in (0, 1) if n % 2 == 0 else (2, 3):
                    s, a = j % 2, j // 2
                    h = 4 * g + j
                    rows = slice(32 * j, 32 * j + 32)
                    p0 = prob[:, (sg * UNITS + 2 * gg + s) % P_RING, a * S:(a + 1) * S]
                    p1 = prob[:, (sg * UNITS + 4 + s) % P_RING, (2 * gg + a) * P:(2 * gg + a + 1) * P]
                    pe.matmul(ps[rows, PVB, col:col + S], v_aug[:, b % 2, 0, h, :], p0, start=True, stop=True,
                              skip_group_check=True)
                    mm = pe.matmul(ps[rows, PVB, col + P:col + S], v_aug[:, b % 2, 1, h, :], p1,
                                   start=False, stop=True, skip_group_check=True)
                if n % 4 == 3:
                    mm.then_inc(pv_done, 1)

            def output(b, t):
                bank = claim(("O", b, t))
                pe.wait_ge(o_evac, 2 * (b + 1))
                for g in range(4):
                    tr = pe.transpose(ps[:, bank, g * P:(g + 1) * P], o_t[:, g, t * P:(t + 1) * P], ident[:, :])
                tr.then_inc(work_full, 1)

            def tokens_t(b):
                bank = claim(("Y", b, 0))
                pe.wait_ge(y_ready, TB * (b + 1))
                for k in range(KD):
                    for t in range(TB):
                        tr = pe.transpose(ps[:, bank, (TB * k + t) * P:(TB * k + t + 1) * P],
                                          y[:, TB * b + t, k * P:(k + 1) * P], ident[:, :])
                tr.then_inc(work_full, 1)

            def router_logits(part):
                lo, hi = PARTS[part]
                bank = claim(("L", part, 0))
                pe.wait_ge(*emptied[slot_of[("Y", (hi - 1) // TB, 0)]])
                for i in range(lo, hi):
                    for k in range(KD):
                        for half in (y_hi, y_lo):
                            mm = pe.matmul(ps[:, bank, (i - lo) * 2 * E:(i - lo + 1) * 2 * E],
                                           half[:, k, i * P:(i + 1) * P], wr_t[:, k, :],
                                           start=(k == 0 and half is y_hi), stop=(k == KD - 1 and half is y_lo))
                mm.then_inc(work_full, 1)

            def scores_tr(part, n):
                bank = claim(("R", part, n))
                pe.wait_ge(score_ready, part + 1)
                for j, i in enumerate(range(*PARTS[part])):
                    tr = pe.transpose(ps[:, bank, j * P:(j + 1) * P], score_st[:, i, :].bitcast(F32), ident[:, :])
                tr.then_inc(work_full, 1)

            pe.wait_ge(consts, 1)
            pe.wait_ge(small_in, 96)
            for k in range(KD):
                pe.transpose(ps[:, 7, k * E:(k + 1) * E], wr_sb[:, k * P:(k + 1) * P], ident[0:E, 0:E])
            for g in range(2):
                for f in range(FD):
                    at = KD * E + (g * FD + f) * E
                    tr = pe.transpose(ps[:, 7, at:at + E], bgu_sb[:, 2 * f * P + g:2 * (f + 1) * P:2],
                                      ident[0:E, 0:E])
            tr.then_inc(small_t, 1)
            for kind, b, n in steps:
                if kind == "T":
                    stacks_t(b, n)
                elif kind == "X":
                    row_scores(b, n)
                elif kind == "M":
                    maxima_t(b)
                elif kind == "S":
                    scores(b, n)
                elif kind == "V":
                    weigh(b, n)
                elif kind == "O":
                    output(b, n)
                elif kind == "Y":
                    tokens_t(b)
                elif kind == "L":
                    router_logits(b)
                elif kind == "R":
                    scores_tr(b, n)

            def gate_up(e, par, c):
                n = CH * e + c
                tg, f = c // FD, c % FD
                b0 = 2 * (c % 2)
                fwait(pe, u_ready, n - 1)
                if c == 0:
                    pe.wait_ge(w_hi, 2 * e + 1)
                    pe.wait_ge(w_lo, 3 * e + 2)
                tok = slice(tg * GRP, (tg + 1) * GRP)
                for g in range(2):
                    for k in range(KD):
                        hi = gu_hi[:, par, k, g, f * P:(f + 1) * P]
                        lo = gu_lo[:, par, k, g, f * P:(f + 1) * P]
                        o = ps[:, b0 + g, :]
                        pe.matmul(o, hi, y_hi[:, k, tok], start=(k == 0), stop=False)
                        pe.matmul(o, hi, y_lo[:, k, tok], start=False, stop=False)
                        mm = pe.matmul(o, lo, y_hi[:, k, tok], start=False, stop=(k == KD - 1))
                mm.then_inc(gu_done, 1)

            def down(n, e, par, c):
                tg, f = c // FD, c % FD
                pe.wait_ge(hlo_ready, n + 1)
                pe.wait_ge(w_lo, 3 * e + 3)
                for m in range(KD):
                    hi = dn_hi[:, par, f, m * P:(m + 1) * P]
                    lo = dn_lo[:, par, f, m * P:(m + 1) * P]
                    o = ps[:, acc_bank(tg, m), :]
                    pe.matmul(o, hi, h_hi[:, c, :], start=False, stop=True, skip_group_check=True)
                    pe.matmul(o, hi, h_lo[:, c, :], start=False, stop=True, skip_group_check=True)
                    mm = pe.matmul(o, lo, h_hi[:, c, :], start=False, stop=True, skip_group_check=True)
                mm.then_inc(dn_done, 1)

            def select_scores():
                pe.wait_ge(consts, 17)
                for e in range(2):
                    pe.matmul(ps[:, acc_bank(1, e), :], sel[:, e, :], score_sT[:, GRP:T], start=True, stop=True
                              ).then_inc(sel_full, 1)

            def bias_terms(tg):
                for m in range(KD):
                    pe.matmul(ps[:, acc_bank(tg, m), :], bdn_st[:, m * P:(m + 1) * P],
                              score_sT[:, tg * GRP:(tg + 1) * GRP], start=True, stop=True, skip_group_check=True)

            def expert(e, par, first):
                for c in range(CH):
                    n = CH * e + c
                    if first and c == 0:
                        pe.wait_ge(exp_done, 2 * B * UNITS)
                    if first and c == 2:
                        router_logits(1)
                    gate_up(e, par, c)
                    if first and c == 1:
                        tokens_t(B - 1)
                    if first and c == 2:
                        pe.wait_ge(*emptied[slot_of[("R", 0, 0)]])
                        pe.wait_ge(*emptied[attention_last[6]])
                        pe.wait_ge(o_evac, 2 * B)
                        bias_terms(0)
                    if first and c == 3:
                        scores_tr(1, 0)
                        pe.wait_ge(*emptied[slot_of[("R", 1, 0)]])
                        select_scores()
                    if c >= 2:
                        down(n - 2, e, par, c - 2)
                    elif not first:
                        down(n - 2, e - 1, 1 - par, c + 2)
                    if first and c == 3:
                        pe.wait_ge(score_sel, 2)
                        bias_terms(1)

            expert(0, 0, True)
            expert(1, 1, False)
            with pe.Fori(1, E // 2) as i:
                expert(2 * i, 0, False)
                expert(2 * i + 1, 1, False)
            down(CH * E - 2, E - 1, 1, 2)

            def outputs_back(j):
                tg = j // 2
                pe.wait_ge(u_ready, CH * E)
                pe.wait_ge(outt_ready[0], tg + 1)
                pe.wait_ge(outt_ready[1], tg + 1)
                for a in range(2):
                    for m in range(KD):
                        col = ((2 * j + a) % 4) * P
                        tr = pe.transpose(ps[:, j, (a * KD + m) * P:(a * KD + m + 1) * P],
                                          out_t[:, tg, m, col:col + P], ident[:, :])
                tr.then_inc(out_tr, 1)

            outputs_back(0)
            outputs_back(1)
            down(CH * E - 1, E - 1, 1, 3)
            outputs_back(2)
            outputs_back(3)


_INS = ['x', 'ctx_2048', 'L0_ffn_router_weight', 'L0_ffn_router_bias', 'L0_ffn_gate_up_proj',
        'L0_ffn_gate_up_proj_bias', 'L0_ffn_down_proj', 'L0_ffn_down_proj_bias']


def kernel(**inputs):
    import numpy as _np
    import concourse.bacc as _bacc
    from concourse import mybir as _mybir
    from concourse.bass_utils import run_bass_kernel_spmd as _run

    nc = _bacc.Bacc("TRN2", target_bir_lowering=False, num_devices=1)
    arrays, args = {}, []
    for name in _INS:
        a = _np.ascontiguousarray(inputs[name])
        arrays[f"in_{name}_dram"] = a
        args.append(nc.dram_tensor(f"in_{name}_dram", a.shape, _mybir.dt.from_np(a.dtype), kind="ExternalInput").ap())
    tokens = args[0].shape[0] * args[0].shape[1]
    scores = nc.dram_tensor("scores_dram", (args[2].shape[0], tokens), _mybir.dt.float32, kind="Internal").ap()
    out = nc.dram_tensor("out_0_dram", args[0].shape, _mybir.dt.float32, kind="ExternalOutput").ap()
    xattn_moe(nc, *args, scores, out)
    r = _run(nc, [arrays], core_ids=[0])
    return r.results[0]["out_0_dram"]
```

```python
import math
from contextlib import ExitStack

import concourse.bass as bass
from concourse import mybir

F32 = mybir.dt.float32
F32R = mybir.dt.float32r
BF16 = mybir.dt.bfloat16
U32 = mybir.dt.uint32
ALU = mybir.AluOpType
ACT = mybir.ActivationFunctionType
AX = mybir.AxisListType

P = 128
NEG = -1.0e30
EPS = 1e-5
ALPHA = 1.702
LIMIT = 7.0
TOP_K = 4
WARM_UP = 36


def xattn_moe(nc, x, ctx_in, w_router, b_router, w_gu, b_gu, w_dn, b_dn, score_dram, out):
    B, S, D = x.shape
    E = w_router.shape[0]
    H = 16
    HD = D // H
    PAIRS = H // 2
    T = B * S
    NT = T // P
    TB = S // P
    KD = D // P
    F = w_dn.shape[1]
    FD = F // P
    SC = 1.0 / HD ** 0.5
    ST = 64
    GRP = 512
    NG = T // GRP
    CH = NG * FD
    UNITS = 6
    ST_RING, P_RING = 4, 12
    assert (B, TB, KD, FD, NG) == (4, 2, 2, 2, 2)

    with ExitStack() as es:
        def sb(name, shape, dt=F32):
            return es.enter_context(nc.sbuf_tensor(name, shape, dt))

        def sem(name):
            return es.enter_context(nc.semaphore(name))

        ps = es.enter_context(nc.psum_tensor("ps", [P, 8, 512], F32))
        SCORE, WORK, PVB = (0, 1, 2, 3), (4, 5, 6), 7

        ident = sb("ident", [P, P])
        ident_b = sb("ident_b", [P, P], BF16)
        mask_diag = sb("mask_diag", [P, 4, P], BF16)
        iota_e = sb("iota_e", [P, E])

        euler = sb("euler", [P, NT // 2, TOP_K - 1])
        sel_f = sb("sel_f", [P, 2, P])
        sel = sb("sel", [P, 2, P], F32R)

        x_tok = sb("x_tok", [P, NT, D])
        ctx_tok = sb("ctx_tok", [P, NT, D])
        stats = sb("stats", [P, NT, 6])
        mv = sb("mv", [P, NT, 2])
        neg_half = sb("neg_half", [P, TB])
        var_eps = sb("var_eps", [P, 2, NT])
        rstd = sb("rstd", [P, 2, NT])
        q_norm = sb("q_norm", [P, 2, TB, D])
        q_stack = sb("q_stack", [P, 2, TB, H, ST], F32R)
        k_stack = sb("k_stack", [P, 2, TB, H, ST], F32R)
        q_t = sb("q_t", [P, 2, PAIRS, S], F32R)
        k_t = sb("k_t", [P, 2, PAIRS, 2, S], F32R)
        v_aug = sb("v_aug", [P, 2, TB, H, 32])
        neg_max = sb("neg_max", [P, 2, TB, 2, 2, 4])
        max_t = sb("max_t", [PAIRS, 2, 2, S], F32R)
        prob = sb("prob", [P, P_RING, 512])
        o_t = sb("o_t", [P, 4, S])
        r_den = sb("r_den", [P, TB, H])
        attn = sb("attn", [P, TB, D])

        y = ctx_tok
        y_hi = k_t[:, 0, 0:4, :, :].rearrange("p (k a) h s -> p k (a h s)", k=KD)
        y_lo = k_t[:, 0, 4:8, :, :].rearrange("p (k a) h s -> p k (a h s)", k=KD)
        wr_sb = sb("wr_sb", [E, D])
        br_sb = sb("br_sb", [P, E])
        wr_t = sb("wr_t", [P, KD, 2 * E], F32R)
        bgu_sb = sb("bgu_sb", [E, 2 * F])
        bias_g = sb("bias_g", [P, FD, E])
        bias_u = sb("bias_u", [P, FD, E])
        bdn_raw = sb("bdn_raw", [3 * E, D])
        bdn_tmp = sb("bdn_tmp", [3 * E, D], F32R)
        bdn_st = sb("bdn_st", [P, D], F32R)
        lg2 = sb("lg2", [P, NT, 2 * E])
        logits = sb("logits", [P, NT, E])
        top8 = sb("top8", [P, NT, 8])
        idx8 = sb("idx8", [P, NT, 8], U32)
        idx_f = sb("idx_f", [P, NT, TOP_K])
        top_d = sb("top_d", [P, NT, TOP_K])
        top_e = sb("top_e", [P, NT, TOP_K])
        top_s = sb("top_s", [P, NT])
        top_r = sb("top_r", [P, NT])
        top_w = sb("top_w", [P, NT, TOP_K])
        onehot = sb("onehot", [P, NT * TOP_K, E])
        onehot_w = sb("onehot_w", [P, NT * TOP_K, E])
        score_st = sb("score_st", [P, NT, P], F32R)
        score_sT = sb("score_sT", [P, T], F32R)
        score_t = sb("score_t", [64 + E, T])
        score_b = q_stack[:, 0, :, :, :].bitcast(F32).rearrange("p t h c -> p t (h c)")

        raw_gu = sb("raw_gu", [P, 2, KD, 2 * F])
        raw_dn = sb("raw_dn", [P, 2, FD, D])
        out_t = raw_gu
        out_sb = ctx_tok
        gu_hi = sb("gu_hi", [P, 2, KD, 2, F], F32R)
        gu_lo = sb("gu_lo", [P, 2, KD, 2, F], F32R)
        dn_hi = sb("dn_hi", [P, 2, FD, D], F32R)
        dn_lo = sb("dn_lo", [P, 2, FD, D], F32R)
        hid, gate, sig = prob[:, 0:4, :], prob[:, 4:6, :], prob[:, 6:8, :]
        glu, up = prob[:, 8:10, :], prob[:, 10:12, :]
        up_s = q_norm.rearrange("p a t d -> p a (t d)")
        h_hi = q_t[:, 0, :, :].rearrange("p (c a) s -> p c (a s)", c=CH)
        h_lo = q_t[:, 1, :, :].rearrange("p (c a) s -> p c (a s)", c=CH)

        x_in = [sem(f"x_in{b}") for b in range(B)]
        ctx_dma = [sem(f"ctx_in{b}") for b in range(B)]
        small_in = sem("small_in")
        v_pads = sem("v_pads")
        small_pads = sem("small_pads")
        consts = sem("consts")
        pool_step = sem("pool_step")
        dve_step = sem("dve_step")
        var_ready = sem("var_ready")
        rstd_ready = sem("rstd_ready")
        k_pads0 = sem("k_pads0")
        k_pads = sem("k_pads")
        small_t = sem("small_t")
        small_done = sem("small_done")
        q_norm_ready = sem("q_norm_ready")
        stack_hi = sem("stack_hi")
        stack_dup = sem("stack_dup")
        stack_lo = sem("stack_lo")
        v_ready = sem("v_ready")
        work_full = sem("work_full")
        work_act = sem("work_act")
        work_dve = sem("work_dve")
        max_rows = [[sem(f"max_rows{p}{h}") for h in range(2)] for p in range(2)]
        st_full = sem("st_full")
        exp_done = sem("exp_done")
        sel_done = sem("sel_done")
        pv_done = sem("pv_done")
        o_evac = sem("o_evac")
        y_ready = sem("y_ready")
        topd_ready = sem("topd_ready")
        tope_ready = sem("tope_ready")
        score_ready = sem("score_ready")
        score_sT_ready = sem("score_sT_ready")
        score_out = sem("score_out")
        yhi_ready = sem("yhi_ready")
        score_in = [[sem(f"score_in{p}{g}") for g in range(NG)] for p in range(2)]
        sel_full = sem("sel_full")
        score_sel = sem("score_sel")
        raw_in = [sem("raw_in0"), sem("raw_in1")]
        w_hi = sem("w_hi")
        w_lo = sem("w_lo")
        gu_done = sem("gu_done")
        g_ready = sem("g_ready")
        u_ready = sem("u_ready")
        us_ready = sem("us_ready")
        sig_ready = sem("sig_ready")
        glu_ready = sem("glu_ready")
        h_ready = sem("h_ready")
        hhi_ready = sem("hhi_ready")
        hlo_ready = sem("hlo_ready")
        dn_done = sem("dn_done")
        outt_ready = [sem("outt_act"), sem("outt_dve")]
        out_tr = sem("out_tr")
        out_ready = sem("out_ready")
        out_dma = sem("out_dma")

        def fwait(eng, s, n):
            if not isinstance(n, int) or n > 0:
                eng.wait_ge(s, n)

        def slot(b):
            def of(kind, batch, numbers):
                return [(kind, batch, n) for n in numbers]

            old = b - 1
            if b + 1 < B:
                new = b + 1
                order = [("T", new, (0, 1, 2)), ("V", old, (4,)), ("T", new, (3, 4, 5)), ("V", old, (5,)),
                         ("S", b, (0,)), ("V", old, (6,)), ("T", new, (6,)), ("V", old, (7,)),
                         ("X", new, (0, 1, 2)), ("S", b, (1,)), ("X", new, (3,)), ("S", b, (2,)),
                         ("X", new, (4,)), ("O", old, (0, 1)), ("T", new, (7,)), ("S", b, (3, 4)),
                         ("X", new, (5, 6, 7)), ("V", b, (0,)), ("M", new, (0,)), ("X", new, (8, 9)),
                         ("V", b, (1,)), ("X", new, (10, 11)), ("S", b, (5,)), ("V", b, (2, 3)),
                         ("M", new, (1,))]
            else:
                order = [("Y", 0, (0,)), ("S", b, (0,)), ("V", old, (4, 5, 6, 7)), ("Y", 1, (0,)),
                         ("S", b, (1,)), ("O", old, (0, 1)), ("S", b, (2, 3)), ("L", 0, (0,)), ("S", b, (4,)),
                         ("V", b, (0,)), ("S", b, (5,)), ("V", b, (1, 2, 3, 4, 5, 6, 7)), ("R", 0, (0,)),
                         ("O", b, (0, 1)), ("Y", 2, (0,))]
            return [u for kind, batch, numbers in order if batch >= 0 for u in of(kind, batch, numbers)]

        first = (("T", (0, 1, 2, 3, 4, 5)), ("X", (0, 1)), ("T", (6,)), ("X", (2, 3)), ("T", (7,)),
                 ("X", (4, 5, 6, 7, 8, 9, 10, 11)), ("M", (0, 1)))
        steps = [(kind, 0, n) for kind, numbers in first for n in numbers]
        for b in range(B):
            steps += [u for u in slot(b) if u not in steps]
        late = [("Y", B - 1, 0), ("L", 1, 0), ("R", 1, 0)]
        PARTS = [(0, NT // 2), (NT // 2, NT)]

        def t_use(n):
            return (n // 2) % 2, n // 4, n % 2

        def x_use(n):
            half, n = n // 6, n % 6
            if n < 2:
                return 0, n, 4 * half, 4, P
            n -= 2
            return 1, n // 2, 4 * half + 2 * (n % 2), 2, S

        def st_unit(i):
            if i < 4:
                return i % 2, 2 * (i // 2), 2, 0, 0
            return i % 2, 0, 4, 1, P

        uses = [u for u in steps + late if u[0] in "TXMOYLR"]
        slot_of = {u: i for i, u in enumerate(uses)}

        def by_act(n):
            return t_use(n)[2] == 1 or n == 0

        emptied = []
        n_act = n_dve = 0
        for kind, b, n in uses:
            if (kind, b) == ("R", 1):
                n_act += 1
                emptied.append((work_act, n_act))
            elif kind == "T" and by_act(n):
                n_act += 1 + t_use(n)[2]
                emptied.append((work_act, n_act))
            elif kind == "O" and n == 0:
                emptied.append(None)
            else:
                if kind == "O":
                    n_dve += 1
                    emptied[slot_of[("O", b, 0)]] = (work_dve, n_dve)
                n_dve += 1
                emptied.append((work_dve, n_dve))
        bank_of, before = [], []
        last_use = {}
        free, preamble, attention_last = WORK + SCORE, None, None
        for u in steps + late:
            if u[0] == "S" and preamble is None:
                free, preamble = WORK, dict(last_use)
            if u == late[0]:
                free, attention_last = WORK[:2], dict(last_use)
            if u in slot_of:
                bank = min(free, key=lambda k: last_use.get(k, -1))
                bank_of.append(bank)
                before.append(last_use.get(bank))
                last_use[bank] = slot_of[u]

        def work_bank(use):
            return bank_of[slot_of[use]]

        def acc_bank(tg, m):
            return (6, 4)[tg] + m

        def stack_low(eng, b):
            par = b % 2
            eng.wait_ge(stack_hi, 2 * b + 2)
            eng.wait_ge(q_norm_ready, TB * (b + 1))
            src_q = q_norm[:, par, :, :].rearrange("p t (h d) -> p (t h) d", h=H)
            src_k = ctx_tok[:, TB * b:TB * b + TB, :].rearrange("p t (h d) -> p (t h) d", h=H)
            qs = q_stack[:, par, :, :, :].rearrange("p t h c -> p (t h) c")
            ks = k_stack[:, par, :, :, :].rearrange("p t h c -> p (t h) c")
            eng.tensor_tensor(ks[:, :, 48:64], src_k, ks[:, :, 0:16].bitcast(F32), ALU.subtract
                              ).then_inc(stack_lo, 1)
            eng.tensor_tensor(qs[:, :, 16:32], src_q, qs[:, :, 0:16].bitcast(F32), ALU.subtract
                              ).then_inc(stack_lo, 1)

        def queries_out(eng, b, n):
            t, half, _ = t_use(n)
            u = ("T", b, n)
            eng.wait_ge(work_full, slot_of[u] + 1)
            if b >= 2:
                eng.wait_ge(st_full, 2 * UNITS * (b - 1))
            dst = q_t[:, b % 2, 4 * half:4 * half + 4, t * P:(t + 1) * P]
            src = ps[:, work_bank(u), :].rearrange("p (a q) -> p a q", a=4)
            if by_act(n):
                eng.activation(dst, src, ACT.Copy).then_inc(work_act, 1)
            else:
                eng.tensor_copy(dst, src).then_inc(work_dve, 1)

        def scores_out(copy, part, emptier):
            u = ("R", part, 0)
            lo, hi = PARTS[part]
            cols, w = slice(lo * P, hi * P), (hi - lo) * P
            copy(score_sT[:, cols], ps[:, work_bank(u), 0:w]).then_inc(score_sT_ready, 1)
            copy(score_t[64:64 + E, cols], ps[64:64 + E, work_bank(u), 0:w]).then_inc(emptier, 1)

        block = es.enter_context(nc.Block())

        @block.sync
        def _(sp):
            def load_weights(e, par):
                sp.dma_start(raw_gu[:, par, :, :], w_gu[e].rearrange("(k p) n -> p k n", p=P)
                             ).then_inc(raw_in[par], 16)
                sp.dma_start(raw_dn[:, par, :, :], w_dn[e].rearrange("(k p) n -> p k n", p=P)
                             ).then_inc(raw_in[par], 16)

            def load_scores(e, par, tg):
                sp.dma_start(score_b[:, par, tg * GRP:(tg + 1) * GRP],
                             score_dram[e, tg * GRP:(tg + 1) * GRP].partition_broadcast(P)
                             ).then_inc(score_in[par][tg], 16)

            for b in range(B):
                sp.dma_start(x_tok[:, TB * b:TB * b + TB, :], x[b].rearrange("(t p) d -> p t d", p=P)
                             ).then_inc(x_in[b], 16)
                if b >= 1:
                    sp.dma_start(ctx_tok[:, TB * b:TB * b + TB, :], ctx_in[b].rearrange("(t p) d -> p t d", p=P)
                                 ).then_inc(ctx_dma[b], 16)
            sp.dma_start(wr_sb[:, :], w_router[:, :]).then_inc(small_in, 16)
            sp.dma_start(bgu_sb[:, :], b_gu[:, :]).then_inc(small_in, 16)
            sp.dma_start(br_sb[:, :], b_router.partition_broadcast(P)).then_inc(small_in, 16)
            for j in range(3):
                sp.dma_start(bdn_raw[j * E:(j + 1) * E, :], b_dn[:, :]).then_inc(small_in, 16)
            load_weights(0, 0)
            load_weights(1, 1)
            for b in range(B):
                for half in range(2):
                    sp.wait_ge(*emptied[slot_of[("M", b, half)]])
                    for s in range(2):
                        sp.dma_start(q_t[64 * s + 32:64 * s + 33, b % 2, 4 * half:4 * half + 4, :].bitcast(F32),
                                     max_t[4 * s:4 * s + 4, b % 2, half, :].bitcast(F32)
                                     ).then_inc(max_rows[b % 2][half], 16)
            for part in range(2):
                lo, hi = PARTS[part]
                sp.wait_ge(*emptied[slot_of[("R", part, 0)]])
                sp.dma_start(score_dram[:, lo * P:hi * P], score_t[64:64 + E, lo * P:hi * P]
                             ).then_inc(score_out, 16)
                sp.wait_ge(score_out, 16 * (part + 1))
                if part == 0:
                    for par in range(2):
                        load_scores(par, par, 0)
            with sp.Fori(0, E // 2 - 1) as i:
                for par in range(2):
                    e = 2 * i + par
                    sp.wait_ge(w_hi, 2 * e + 2)
                    sp.wait_ge(w_lo, 3 * e + 3)
                    load_weights(e + 2, par)
                    for tg in range(NG):
                        sp.wait_ge(us_ready, CH * e + FD * (tg + 1))
                        load_scores(e + 2, par, tg)
            for j in range(4):
                sp.wait_ge(out_ready, j + 1)
                sp.dma_start(out[j].rearrange("(t p) d -> p t d", p=P), out_sb[:, 2 * j:2 * j + 2, :]
                             ).then_inc(out_dma, 16)
            sp.wait_ge(out_dma, 64)

        @block.gpsimd
        def _(pool):
            done = [0]

            def step(ins):
                done[0] += 1
                ins.then_inc(pool_step, 1)

            def settle():
                pool.wait_ge(pool_step, done[0])

            step(pool.memset(ident[:, :], 0.0))
            settle()
            pool.affine_select(out=ident[:, :], in_=ident[:, :], compare_op=ALU.not_equal, fill=1.0, base=0,
                               pattern=[[-1, P]], channel_multiplier=1).then_inc(consts, 1)
            step(pool.memset(neg_half[:, :], -0.5))
            step(pool.memset(euler[:, :, :], math.e))
            step(pool.memset(top_e[:, NT // 2:NT, 0:1], 1.0))

            def rsqrt(b, which):
                pool.wait_ge(var_ready, B * which + b + 1)
                t = slice(TB * b, TB * b + TB)
                pool.tensor_tensor(rstd[:, which, t], var_eps[:, which, t], neg_half[:, :], ALU.pow
                                   ).then_inc(rstd_ready, 1)

            def stack_pads(par):
                for t in range(TB):
                    pool.memset(q_stack[:, par, t, :, 32:48].bitcast(F32), 0.0).then_inc(consts, 1)
                    pool.memset(k_stack[:, par, t, :, 32:48].bitcast(F32), 0.0).then_inc(consts, 1)
                pool.wait_ge(consts, (1, 9)[par] + 2 * TB)
                for t in range(TB):
                    pool.memset(k_stack[:, par, t, :, 32:33].bitcast(F32), 1.0).then_inc(consts, 1)

            def dup(b):
                par = b % 2
                pool.wait_ge(stack_hi, 2 * b + 2)
                qs = q_stack[:, par, :, :, :].rearrange("p t h c -> p (t h) c")
                ks = k_stack[:, par, :, :, :].rearrange("p t h c -> p (t h) c")
                pool.tensor_scalar(qs[:, :, 48:64], qs[:, :, 0:16].bitcast(F32), 1.0, 1.0, ALU.mult, ALU.mult
                                   ).then_inc(stack_dup, 1)
                pool.tensor_scalar(ks[:, :, 16:32], ks[:, :, 0:16].bitcast(F32), 1.0, 1.0, ALU.mult, ALU.mult
                                   ).then_inc(stack_dup, 1)

            def values(b):
                pool.wait_ge(ctx_dma[b], 16)
                if b >= 2:
                    pool.wait_ge(pv_done, 2 * (b - 1))
                for t in range(TB):
                    pool.tensor_scalar(v_aug[:, b % 2, t, :, 0:HD],
                                       ctx_tok[:, TB * b + t, :].rearrange("p (h d) -> p h d", h=H),
                                       1.0, 1.0, ALU.mult, ALU.mult).then_inc(v_ready, 1)

            def select(u):
                pool.wait_ge(exp_done, u + 1)
                w, n = (S, 2) if u % UNITS < 4 else (P, 4)
                blk = prob[:, u % P_RING, :].rearrange("p (h q) -> p h q", q=w)[:, :, 0:P]
                pool.affine_select(out=blk, in_=blk, compare_op=ALU.is_ge, fill=0.0, base=0,
                                   pattern=[[0, n], [1, P]], channel_multiplier=-1).then_inc(sel_done, 1)

            def top_powers():
                lo, hi = PARTS[1]
                pool.wait_ge(topd_ready, 2)
                pool.tensor_tensor(top_e[:, lo:hi, 1:TOP_K], euler[:, :, :], top_d[:, lo:hi, 1:TOP_K], ALU.pow
                                   ).then_inc(tope_ready, 1)

            def lo_gu(e, par, k):
                pool.wait_ge(w_hi, 2 * e + 1)
                pool.tensor_tensor(gu_lo[:, par, k, :, :],
                                   raw_gu[:, par, k, :].rearrange("p (d g) -> p g d", g=2),
                                   gu_hi[:, par, k, :, :].bitcast(F32), ALU.subtract).then_inc(w_lo, 1)

            def lo_dn(e, par):
                pool.wait_ge(w_hi, 2 * e + 2)
                pool.tensor_tensor(dn_lo[:, par, :, :], raw_dn[:, par, :, :],
                                   dn_hi[:, par, :, :].bitcast(F32), ALU.subtract).then_inc(w_lo, 1)

            def key_pads(par, v):
                rows = slice(64 - 64 * v, 128 - 64 * v)
                pool.memset(k_t[rows, par, :, v, :].bitcast(F32), 0.0).then_inc(k_pads, 1)

            stack_pads(0)
            settle()
            rsqrt(0, 0)
            dup(0)
            pool.wait_ge(stack_dup, 2)
            key_pads(0, 1)
            pool.wait_ge(k_pads, 1)
            step(pool.memset(ident_b[:, :], 0.0))
            step(pool.memset(mask_diag[:, :, :], 0.0))
            settle()
            pool.affine_select(out=ident_b[:, :], in_=ident_b[:, :], compare_op=ALU.not_equal, fill=1.0, base=0,
                               pattern=[[-1, P]], channel_multiplier=1).then_inc(consts, 1)
            pool.affine_select(out=mask_diag[:, :, :], in_=mask_diag[:, :, :], compare_op=ALU.is_ge, fill=NEG,
                               base=0, pattern=[[0, 4], [-1, P]], channel_multiplier=1).then_inc(consts, 1)
            for b in range(1, B):
                rsqrt(b, 0)
            pool.memset(v_aug[:, :, :, :, HD:32].rearrange("p a t h c -> p (a t h) c"), 0.0).then_inc(v_pads, 1)
            pool.wait_ge(v_pads, 1)
            pool.memset(v_aug[:, :, :, :, HD:HD + 1].rearrange("p a t h c -> p (a t h) c"), 1.0
                        ).then_inc(v_pads, 1)
            stack_pads(1)
            dup(1)
            stack_low(pool, 1)
            pool.wait_ge(stack_lo, 4)
            for v in range(2):
                key_pads(1, v)
                pool.wait_ge(k_pads, v + 2)
            values(0)
            pool.iota(iota_e[:, :], pattern=[[1, E]], base=0, channel_multiplier=0,
                      allow_small_or_imprecise_dtypes=True).then_inc(consts, 1)
            step(pool.memset(sel_f[:, :, :], 0.0))
            for row in (0, E):
                settle()
                step(pool.affine_select(out=sel_f[:, :, :], in_=sel_f[:, :, :], compare_op=ALU.not_equal, fill=1.0,
                                        base=-row, pattern=[[-1, 2], [0, P]], channel_multiplier=1))
            settle()
            pool.tensor_scalar(sel[:, :, :], sel_f[:, :, :], 1.0, 1.0, ALU.mult, ALU.mult).then_inc(consts, 1)
            values(1)
            pool.memset(bdn_st[:, :].bitcast(F32), 0.0).then_inc(small_pads, 1)
            pool.memset(score_st[:, :, :].bitcast(F32), 0.0).then_inc(small_pads, 1)
            for kind, b, n in steps:
                if kind == "S":
                    u = 2 * UNITS * b + 2 * n
                    select(u)
                    select(u + 1)
                    if n == 2 and 2 <= b + 1 < B:
                        values(b + 1)
                    if n == 4 and b >= 1:
                        rsqrt(b - 1, 1)
                    if n in (4, 5) and b == 1:
                        lo_gu(0, 0, n - 4)
                    if n == 2 and b + 2 < B:
                        dup(b + 2)
                        stack_low(pool, b + 2)
                    if n == 3 and b == 2:
                        lo_dn(0, 0)
            rsqrt(B - 1, 1)

            def expert(e, par, first, last):
                for c in range(CH):
                    n = CH * e + c
                    pool.wait_ge(sig_ready, n + 1)
                    fwait(pool, h_ready, n - 1)
                    pool.tensor_tensor(glu[:, c % 2, :], gate[:, c % 2, :], sig[:, c % 2, :],
                                       ALU.mult).then_inc(glu_ready, 1)
                    if first and c == 1:
                        top_powers()
                    if not last and c < 2:
                        lo_gu(e + 1, 1 - par, c)
                    if not last and c == (3 if first else 2):
                        lo_dn(e + 1, 1 - par)

            expert(0, 0, True, False)
            expert(1, 1, False, False)
            with pool.Fori(1, E // 2 - 1) as i:
                expert(2 * i, 0, False, False)
                expert(2 * i + 1, 1, False, False)
            expert(E - 2, 0, False, False)
            expert(E - 1, 1, False, True)

        @block.scalar
        def _(act):
            act.dma_start(ctx_tok[:, 0:TB, :], ctx_in[0].rearrange("(t p) d -> p t d", p=P)
                          ).then_inc(ctx_dma[0], 16)

            def stack_high(b):
                par = b % 2
                if b >= 2:
                    act.wait_ge(work_full, slot_of[("T", b - 2, 7)] + 1)
                act.wait_ge(ctx_dma[b], 16)
                qs = q_stack[:, par, :, :, :].rearrange("p t h c -> p (t h) c")
                ks = k_stack[:, par, :, :, :].rearrange("p t h c -> p (t h) c")
                act.activation(ks[:, :, 0:16], ctx_tok[:, TB * b:TB * b + TB, :]
                               .rearrange("p t (h d) -> p (t h) d", h=H), ACT.Copy).then_inc(stack_hi, 1)
                act.wait_ge(q_norm_ready, TB * (b + 1))
                act.activation(qs[:, :, 0:16], q_norm[:, par, :, :]
                               .rearrange("p t (h d) -> p (t h) d", h=H), ACT.Copy).then_inc(stack_hi, 1)

            def keys_out(b, n):
                t, half, _ = t_use(n)
                u = ("T", b, n)
                act.wait_ge(work_full, slot_of[u] + 1)
                if b >= 2:
                    act.wait_ge(st_full, 2 * UNITS * (b - 1))
                src = ps[:, work_bank(u), :].rearrange("p (a q) -> p a q", a=4)
                for v in range(2):
                    rows = slice(64 * v, 64 * v + 64)
                    act.activation(k_t[rows, b % 2, 4 * half:4 * half + 4, v, t * P:(t + 1) * P], src[rows],
                                   ACT.Copy).then_inc(work_act, 1)

            def exp_unit(u):
                act.wait_ge(st_full, u + 1)
                if u >= P_RING:
                    act.wait_ge(pv_done, u // UNITS - 1)
                act.activation(prob[:, u % P_RING, :], ps[:, u % ST_RING, :], ACT.Exp,
                               scale=SC).then_inc(exp_done, 1)

            def output_t(b, s2):
                act.wait_ge(pv_done, 2 * b + s2 + 1)
                if b >= 1:
                    act.wait_ge(work_full, slot_of[("O", b - 1, TB - 1)] + 1)
                act.activation(o_t[:, 2 * s2:2 * s2 + 2, :], ps[:, PVB, :].rearrange("p (g q) -> p g q", g=2),
                               ACT.Copy).then_inc(o_evac, 1)

            def tokens_high(b):
                act.wait_ge(work_full, slot_of[("Y", b, 0)] + 1)
                act.activation(y_hi[:, :, b * S:(b + 1) * S],
                               ps[:, work_bank(("Y", b, 0)), :].rearrange("p (k s) -> p k s", k=KD), ACT.Copy
                               ).then_inc(yhi_ready, 1)

            def top_exp():
                lo, hi = PARTS[0]
                act.wait_ge(topd_ready, 1)
                act.activation(top_e[:, lo:hi, :], top_d[:, lo:hi, :], ACT.Exp).then_inc(tope_ready, 1)

            def split_gu(e, par):
                act.activation(gu_hi[:, par, :, :, :], raw_gu[:, par, :, :].rearrange("p k (d g) -> p k g d", g=2),
                               ACT.Copy).then_inc(w_hi, 1)

            def split_dn(e, par):
                act.activation(dn_hi[:, par, :, :], raw_dn[:, par, :, :], ACT.Copy).then_inc(w_hi, 1)

            stack_high(0)
            for kind, b, n in steps:
                if kind == "T" and by_act(n) and t_use(n)[2] == 0:
                    queries_out(act, b, n)
                elif kind == "T" and by_act(n):
                    keys_out(b, n)
                    if b == 0 and n == 7:
                        stack_high(1)
                elif kind == "S":
                    exp_unit(2 * UNITS * b + 2 * n)
                    exp_unit(2 * UNITS * b + 2 * n + 1)
                    if n == 3 and b == 1:
                        act.wait_ge(raw_in[0], 32)
                        split_gu(0, 0)
                    if n == 4 and b == 1:
                        split_dn(0, 0)
                    if n == 2 and b + 2 < B:
                        stack_high(b + 2)
                    if n == 5 and b == B - 1:
                        top_exp()
                elif kind == "V" and n % 4 == 3:
                    output_t(b, n // 4)
                elif kind == "Y":
                    tokens_high(b)

            def high_half(n, c):
                act.wait_ge(h_ready, n + 1)
                fwait(act, dn_done, n - 3)
                act.activation(h_hi[:, c, :], hid[:, c, :], ACT.Copy).then_inc(hhi_ready, 1)

            def expert(e, par, first, last):
                for c in range(CH):
                    n = CH * e + c
                    if first and c == 3:
                        for j in range(2):
                            act.wait_ge(sel_full, j + 1)
                            act.activation(score_b[:, j, GRP:T], ps[:, acc_bank(1, j), :], ACT.Copy
                                           ).then_inc(score_sel, 1)
                    if last and c == CH - 1:
                        high_half(n - 1, c - 1)
                    act.wait_ge(g_ready, n + 1)
                    fwait(act, glu_ready, n - 1)
                    act.activation(sig[:, c % 2, :], gate[:, c % 2, :], ACT.Sigmoid, scale=ALPHA
                                   ).then_inc(sig_ready, 1)
                    if first and c == 0:
                        tokens_high(B - 1)
                    elif not (last and c == CH - 1):
                        if first and c == 2:
                            act.wait_ge(work_full, slot_of[("R", 1, 0)] + 1)
                            scores_out(lambda o, i: act.activation(o, i, ACT.Copy), 1, work_act)
                        high_half(n - 1, (c - 1) % CH)
                    if not last and c == 0:
                        act.wait_ge(raw_in[1 - par], 16 * (e + par) + 32)
                        if not first:
                            act.wait_ge(gu_done, CH * e)
                        split_gu(e + 1, 1 - par)
                    if not last and c == (3 if first else 2):
                        if not first:
                            act.wait_ge(dn_done, CH * e)
                        split_dn(e + 1, 1 - par)

            expert(0, 0, True, False)
            expert(1, 1, False, False)
            with act.Fori(1, E // 2 - 1) as i:
                expert(2 * i, 0, False, False)
                expert(2 * i + 1, 1, False, False)
            expert(E - 2, 0, False, False)
            expert(E - 1, 1, False, True)
            high_half(CH * E - 1, CH - 1)
            for tg in range(NG):
                act.wait_ge(dn_done, CH * E - 2 * (NG - 1 - tg))
                act.activation(out_t[:, tg, 0, :], ps[:, acc_bank(tg, 0), :], ACT.Copy).then_inc(outt_ready[0], 1)

        @block.vector
        def _(dve):
            done = [0]

            def step(ins):
                done[0] += 1
                ins.then_inc(dve_step, 1)

            def settle():
                dve.wait_ge(dve_step, done[0])

            def row_stats(i):
                step(dve.bn_stats(stats[:, i, :], x_tok[:, i, :]))

            def variance(b, which):
                settle()
                for i in range(TB * b, TB * b + TB):
                    step(dve.bn_aggr(mv[:, i, :], stats[:, i, :]))
                settle()
                t = slice(TB * b, TB * b + TB)
                dve.tensor_scalar(var_eps[:, which, t], mv[:, t, 1], EPS, None, ALU.add).then_inc(var_ready, 1)

            def normalise(dst, i, which):
                return dve.tensor_scalar(dst, x_tok[:, i, :], mv[:, i, 0:1], rstd[:, which, i:i + 1],
                                         ALU.subtract, ALU.mult)

            def tokens(b):
                dve.wait_ge(rstd_ready, B + b + 1)
                dve.wait_ge(v_ready, TB * (b + 1))
                for i in range(TB * b, TB * b + TB):
                    normalise(y[:, i, :], i, 1).then_inc(y_ready, 1)

            def queries(b):
                dve.wait_ge(rstd_ready, b + 1)
                if b >= 2:
                    dve.wait_ge(stack_lo, 2 * b - 2)
                for t in range(TB):
                    normalise(q_norm[:, b % 2, t, :], TB * b + t, 0).then_inc(q_norm_ready, 1)

            def row_max(b, n):
                t, s, p0, np_, keys = x_use(n)
                u = ("X", b, n)
                dve.wait_ge(work_full, slot_of[u] + 1)
                if b >= 2 and n == 0:
                    dve.wait_ge(work_full, slot_of[("M", b - 2, 1)] + 1)
                dve.tensor_reduce(neg_max[:, b % 2, t, p0 // 4, s, p0 % 4:p0 % 4 + np_],
                                  ps[:, work_bank(u), :].rearrange("p (a k) -> p a k", k=keys),
                                  AX.X, ALU.max, negate=True).then_inc(work_dve, 1)

            def max_rows_t(b, half):
                u = ("M", b, half)
                dve.wait_ge(work_full, slot_of[u] + 1)
                if b >= 2:
                    dve.wait_ge(max_rows[b % 2][half], 32 * (b // 2))
                dve.tensor_copy(max_t[:, b % 2, half, :], ps[0:PAIRS, work_bank(u), 0:S]).then_inc(work_dve, 1)

            def attn_out(b):
                banks = []
                for t in range(TB):
                    u = ("O", b, t)
                    dve.wait_ge(work_full, slot_of[u] + 1)
                    banks.append(ps[:, work_bank(u), :].rearrange("p (h c) -> p h c", c=32))
                    if t == 0:
                        settle()
                    step(dve.reciprocal(r_den[:, t, :], banks[t][:, :, HD]))
                settle()
                for t in range(TB):
                    dve.tensor_tensor(attn[:, t, :].rearrange("p (h d) -> p h d", h=H), banks[t][:, :, 0:HD],
                                      r_den[:, t, :].unsqueeze(2).to_broadcast([P, H, HD]), ALU.mult
                                      ).then_inc(work_dve, 1)
                for t in range(TB):
                    i = TB * b + t
                    dve.wait_ge(*emptied[slot_of[("O", b, t)]])
                    step(dve.tensor_tensor(x_tok[:, i, :], x_tok[:, i, :], attn[:, t, :], ALU.add))
                settle()
                for t in range(TB):
                    row_stats(TB * b + t)

            def tokens_low(b):
                u = ("Y", b, 0)
                dve.wait_ge(yhi_ready, b + 1)
                cols = slice(b * S, (b + 1) * S)
                dve.tensor_tensor(y_lo[:, :, cols], ps[:, work_bank(u), :].rearrange("p (k s) -> p k s", k=KD),
                                  y_hi[:, :, cols].bitcast(F32), ALU.subtract).then_inc(work_dve, 1)

            def small_weights():
                dve.wait_ge(small_t, 1)
                wr_ps = ps[:, 7, 0:KD * E].rearrange("p (k e) -> p k e", k=KD)
                b_ps = ps[:, 7, KD * E:KD * E + 2 * FD * E].rearrange("p (g f e) -> p g f e", g=2, f=FD)
                step(dve.tensor_copy(wr_t[:, :, 0:E], wr_ps))
                step(dve.tensor_copy(bias_g[:, :, :], b_ps[:, 0, :, :]))
                step(dve.tensor_scalar(bias_u[:, :, :], b_ps[:, 1, :, :], 1.0, None, ALU.add))
                settle()
                dve.tensor_tensor(wr_t[:, :, E:2 * E], wr_ps, wr_t[:, :, 0:E].bitcast(F32), ALU.subtract
                                  ).then_inc(small_done, 1)

            def router_top(part):
                lo, hi = PARTS[part]
                m = hi - lo
                t = slice(lo, hi)
                u = ("L", part, 0)
                if part == 0:
                    dve.wait_ge(consts, 16)
                    dve.wait_ge(small_in, 96)
                dve.wait_ge(work_full, slot_of[u] + 1)
                dve.tensor_copy(lg2[:, t, :], ps[:, work_bank(u), 0:m * 2 * E].rearrange("p (t c) -> p t c", t=m)
                                ).then_inc(work_dve, 1)
                dve.wait_ge(*emptied[slot_of[u]])
                step(dve.tensor_tensor(logits[:, t, :], lg2[:, t, 0:E], lg2[:, t, E:2 * E], ALU.add))
                settle()
                step(dve.tensor_tensor(logits[:, t, :], logits[:, t, :],
                                       br_sb[:, :].unsqueeze(1).to_broadcast([P, m, E]), ALU.add))
                settle()
                for i in range(lo, hi):
                    step(dve.max(top8[:, i, :], logits[:, i, :]))
                settle()
                dve.tensor_tensor(top_d[:, t, :], top8[:, t, 0:TOP_K], top8[:, t, 0:1].to_broadcast([P, m, TOP_K]),
                                  ALU.subtract).then_inc(topd_ready, 1)
                for i in range(lo, hi):
                    step(dve.max_index(idx8[:, i, :], top8[:, i, :], logits[:, i, :]))
                settle()
                step(dve.tensor_copy(idx_f[:, t, :], idx8[:, t, 0:TOP_K]))
                settle()
                tk = slice(lo * TOP_K, hi * TOP_K)
                step(dve.tensor_tensor(onehot[:, tk, :], iota_e[:, :].unsqueeze(1).to_broadcast([P, m * TOP_K, E]),
                                       idx_f[:, t, :].rearrange("p t k -> p (t k)").unsqueeze(2)
                                       .to_broadcast([P, m * TOP_K, E]), ALU.is_equal))

            def router_scores(part):
                lo, hi = PARTS[part]
                m = hi - lo
                t = slice(lo, hi)
                tk = slice(lo * TOP_K, hi * TOP_K)
                dve.wait_ge(tope_ready, part + 1)
                step(dve.tensor_reduce(top_s[:, t], top_e[:, t, :], AX.X, ALU.add))
                settle()
                step(dve.reciprocal(top_r[:, t], top_s[:, t]))
                settle()
                step(dve.tensor_tensor(top_w[:, t, :], top_e[:, t, :],
                                       top_r[:, t].unsqueeze(2).to_broadcast([P, m, TOP_K]), ALU.mult))
                settle()
                step(dve.tensor_tensor(onehot_w[:, tk, :], onehot[:, tk, :],
                                       top_w[:, t, :].rearrange("p t k -> p (t k)").unsqueeze(2)
                                       .to_broadcast([P, m * TOP_K, E]), ALU.mult))
                settle()
                if part == 0:
                    dve.wait_ge(small_pads, 2)
                score = score_st[:, t, 64:64 + E].bitcast(F32)
                step(dve.tensor_reduce(score, onehot_w[:, tk, :].rearrange("p (t k) e -> p t e k", k=TOP_K),
                                       AX.X, ALU.add))
                settle()
                step(dve.tensor_copy(score_st[:, t, 0:E], score))
                step(dve.tensor_copy(score_st[:, t, 2 * E:3 * E], score))
                settle()
                dve.tensor_tensor(score_st[:, t, E:2 * E], score, score_st[:, t, 0:E].bitcast(F32), ALU.subtract
                                  ).then_inc(score_ready, 1)

            dve.memset(k_t[P // 2:P, 0, :, 0, :].bitcast(F32), 0.0).then_inc(k_pads0, 1)
            dve.wait_ge(x_in[0], 16)
            row_stats(0)
            row_stats(1)
            variance(0, 0)
            for b in range(1, B):
                dve.wait_ge(x_in[b], 16)
                for t in range(TB):
                    row_stats(TB * b + t)
                if b == 1:
                    queries(0)
                    stack_low(dve, 0)
            for b in range(1, B):
                variance(b, 0)
            for kind, b, n in steps:
                if kind == "T" and t_use(n)[2] == 0:
                    if not by_act(n):
                        queries_out(dve, b, n)
                    if b == 0 and n == 2:
                        queries(1)
                elif kind == "X":
                    row_max(b, n)
                elif kind == "M":
                    max_rows_t(b, n)
                    if b == 0 and n == 1:
                        small_weights()
                    if b == 1 and n == 1:
                        dve.wait_ge(small_in, 96)
                        dve.wait_ge(small_pads, 1)
                        step(dve.tensor_copy(bdn_tmp[:, :], bdn_raw[:, :]))
                        step(dve.tensor_copy(bdn_st[0:2 * E, :], bdn_raw[0:2 * E, :]))
                        settle()
                        step(dve.tensor_tensor(bdn_st[2 * E:3 * E, :], bdn_raw[2 * E:3 * E, :],
                                               bdn_tmp[2 * E:3 * E, :].bitcast(F32), ALU.subtract))
                elif kind == "O" and n == TB - 1:
                    attn_out(b)
                    variance(b, 1)
                elif kind == "S":
                    if n == 2 and b + 2 < B:
                        queries(b + 2)
                    if n == 5 and b >= 1:
                        tokens(b - 1)
                elif kind == "Y":
                    tokens_low(b)
                elif kind == "L":
                    router_top(b)
                    router_scores(b)
                elif kind == "R":
                    dve.wait_ge(work_full, slot_of[("R", 0, 0)] + 1)
                    scores_out(dve.tensor_copy, 0, work_dve)
            def low_half(n, c):
                dve.wait_ge(hhi_ready, n + 1)
                fwait(dve, dn_done, n - 3)
                dve.tensor_tensor(h_lo[:, c, :], hid[:, c, :], h_hi[:, c, :].bitcast(F32), ALU.subtract
                                  ).then_inc(hlo_ready, 1)

            def hidden(n, c):
                dve.wait_ge(glu_ready, n + 1)
                dve.wait_ge(us_ready, n + 1)
                fwait(dve, hlo_ready, n - 3)
                dve.tensor_tensor(hid[:, c, :], up_s[:, c % 2, :], glu[:, c % 2, :], ALU.mult
                                  ).then_inc(h_ready, 1)

            def gate_out(n, e, c):
                dve.wait_ge(gu_done, n + 1)
                fwait(dve, glu_ready, n - 1)
                dve.tensor_scalar(gate[:, c % 2, :], ps[:, 2 * (c % 2), :], bias_g[:, c % FD, bass.ds(e, 1)], LIMIT,
                                  ALU.add, ALU.min).then_inc(g_ready, 1)

            def up_out(n, e, c):
                fwait(dve, us_ready, n - 1)
                dve.tensor_scalar(up[:, c % 2, :], ps[:, 2 * (c % 2) + 1, :], bias_u[:, c % FD, bass.ds(e, 1)],
                                  LIMIT + 1.0, ALU.add, ALU.min).then_inc(u_ready, 1)

            def up_score(n, e, par, c, ready):
                tg = c // FD
                dve.wait_ge(u_ready, n + 1)
                fwait(dve, h_ready, n - 1)
                if c % FD == 0:
                    dve.wait_ge(*ready)
                dve.scalar_tensor_tensor(up_s[:, c % 2, :], up[:, c % 2, :], 1.0 - LIMIT,
                                         score_b[:, par, tg * GRP:(tg + 1) * GRP], ALU.max, ALU.mult
                                         ).then_inc(us_ready, 1)

            def chunk(n, e, par, c, ready):
                gate_out(n, e, c)
                up_out(n, e, c)
                hidden(n - 1, (c - 1) % CH)
                up_score(n, e, par, c, ready)
                low_half(n - 1, (c - 1) % CH)

            def expert(e, par, chunks):
                for c in range(chunks):
                    tg = c // FD
                    chunk(CH * e + c, e, par, c, (score_in[par][tg], 8 * (e - par) + (16, 0)[tg]))

            N = CH * E
            gate_out(0, 0, 0)
            tokens(B - 1)
            tokens_low(B - 1)
            up_out(0, 0, 0)
            up_score(0, 0, 0, 0, (score_in[0][0], 16))
            gate_out(1, 0, 1)
            up_out(1, 0, 1)
            router_top(1)
            hidden(0, 0)
            up_score(1, 0, 0, 1, None)
            low_half(0, 0)
            gate_out(2, 0, 2)
            router_scores(1)
            up_out(2, 0, 2)
            hidden(1, 1)
            gate_out(3, 0, 3)
            up_out(3, 0, 3)
            low_half(1, 1)
            up_score(2, 0, 0, 2, (score_sel, 1))
            hidden(2, 2)
            up_score(3, 0, 0, 3, None)
            low_half(2, 2)
            for c in range(CH):
                chunk(CH + c, 1, 1, c, (score_in[1][0], 16) if c == 0 else (score_sel, 2))
            with dve.Fori(1, E // 2 - 1) as i:
                expert(2 * i, 0, CH)
                expert(2 * i + 1, 1, CH)
            expert(E - 2, 0, CH)
            expert(E - 1, 1, CH - 1)
            hidden(N - 2, CH - 2)
            gate_out(N - 1, E - 1, CH - 1)
            low_half(N - 2, CH - 2)
            up_out(N - 1, E - 1, CH - 1)
            up_score(N - 1, E - 1, 1, CH - 1, None)
            hidden(N - 1, CH - 1)

            def result_t(tg):
                dve.wait_ge(dn_done, N - 2 * (NG - 1 - tg))
                dve.tensor_copy(out_t[:, tg, 1, :], ps[:, acc_bank(tg, 1), :]).then_inc(outt_ready[1], 1)

            result_t(0)
            low_half(N - 1, CH - 1)
            result_t(1)
            for j in range(4):
                dve.wait_ge(out_tr, j + 1)
                dve.tensor_tensor(out_sb[:, 2 * j:2 * j + 2, :], ps[:, j, :].rearrange("p (t d) -> p t d", t=2),
                                  x_tok[:, 2 * j:2 * j + 2, :], ALU.add).then_inc(out_ready, 1)

        @block.tensor
        def _(pe):
            def claim(use):
                i = slot_of[use]
                if before[i] is not None:
                    pe.wait_ge(*emptied[before[i]])
                return work_bank(use)

            def stacks_t(b, n):
                if n == 0:
                    pe.wait_ge(consts, (7, 15)[b % 2])
                    pe.wait_ge(stack_lo, 2 * b + 2)
                    pe.wait_ge(stack_dup, 2 * b + 2)
                t, half, which = t_use(n)
                bank = claim(("T", b, n))
                src = (q_stack, k_stack)[which]
                for j in range(4):
                    pair = 4 * half + j
                    tr = pe.transpose(ps[:, bank, j * P:(j + 1) * P],
                                      src[:, b % 2, t, 2 * pair:2 * pair + 2, :].bitcast(F32)
                                      .rearrange("p h c -> p (h c)"), ident[:, :])
                tr.then_inc(work_full, 1)

            def row_scores(b, n):
                t, s, p0, np_, keys = x_use(n)
                bank = claim(("X", b, n))
                if n % 6 == 0:
                    for m in range(4):
                        pe.wait_ge(*emptied[slot_of[("T", b, 4 * (n // 6) + m)]])
                if n == 0:
                    pe.wait_ge(k_pads0, 1)
                    pe.wait_ge(k_pads, 2 * min(b, 1) + 1)
                    pe.wait_ge(consts, 9)
                for j in range(np_):
                    pe.matmul(ps[:, bank, j * keys:(j + 1) * keys],
                              q_t[:, b % 2, p0 + j, t * P:(t + 1) * P],
                              k_t[:, b % 2, p0 + j, s, 0:keys], start=(j == 0), stop=True,
                              skip_group_check=True)
                diag = ps[:, bank, :].rearrange("p (a k) -> p a k", k=keys)[:, :, keys - P:keys]
                pe.matmul(diag, ident_b[:, :], mask_diag[:, 0:np_, :], start=False, stop=True,
                          skip_group_check=True).then_inc(work_full, 1)

            def maxima_t(b, half):
                bank = claim(("M", b, half))
                pe.wait_ge(*emptied[slot_of[("X", b, 6 * half + 5)]])
                for t in range(TB):
                    tr = pe.transpose(ps[0:PAIRS, bank, t * P:(t + 1) * P],
                                      neg_max[:, b % 2, t, half, :, :].rearrange("p s a -> p (s a)"), ident[:, :])
                tr.then_inc(work_full, 1)

            def scores(b, n):
                if n % 3 == 0:
                    pe.wait_ge(max_rows[b % 2][n // 3], 32 * (b // 2 + 1))
                u = 2 * UNITS * b + 2 * n
                s2, i = n // 3, 2 * (n % 3)
                fwait(pe, exp_done, u + 2 - ST_RING)
                for v in range(2):
                    if u < ST_RING and u + v in preamble:
                        pe.wait_ge(*emptied[preamble[u + v]])
                    s, p0, np_, kt, q0 = st_unit(i + v)
                    w = S - q0
                    for j in range(np_):
                        pair = 4 * s2 + p0 + j
                        mm = pe.matmul(ps[:, (u + v) % ST_RING, j * w:(j + 1) * w],
                                       k_t[:, b % 2, pair, s, kt * P:(kt + 1) * P],
                                       q_t[:, b % 2, pair, q0:S], start=True, stop=True)
                    mm.then_inc(st_full, 1)

            def weigh(b, n):
                g, gg, s2 = n // 2, (n // 2) % 2, n // 4
                sg = 2 * b + s2
                col = (g % 2) * S
                pe.wait_ge(sel_done, UNITS * (sg + 1))
                pe.wait_ge(v_ready, TB * (b + 1))
                if b == 0 and n == 0:
                    pe.wait_ge(v_pads, 2)
                    pe.wait_ge(small_done, 1)
                if n % 4 == 0:
                    fwait(pe, o_evac, sg)
                for j in (0, 1) if n % 2 == 0 else (2, 3):
                    s, a = j % 2, j // 2
                    h = 4 * g + j
                    rows = slice(32 * j, 32 * j + 32)
                    p0 = prob[:, (sg * UNITS + 2 * gg + s) % P_RING, a * S:(a + 1) * S]
                    p1 = prob[:, (sg * UNITS + 4 + s) % P_RING, (2 * gg + a) * P:(2 * gg + a + 1) * P]
                    pe.matmul(ps[rows, PVB, col:col + S], v_aug[:, b % 2, 0, h, :], p0, start=True, stop=True,
                              skip_group_check=True)
                    mm = pe.matmul(ps[rows, PVB, col + P:col + S], v_aug[:, b % 2, 1, h, :], p1,
                                   start=False, stop=True, skip_group_check=True)
                if n % 4 == 3:
                    mm.then_inc(pv_done, 1)

            def output(b, t):
                bank = claim(("O", b, t))
                pe.wait_ge(o_evac, 2 * (b + 1))
                for g in range(4):
                    tr = pe.transpose(ps[:, bank, g * P:(g + 1) * P], o_t[:, g, t * P:(t + 1) * P], ident[:, :])
                tr.then_inc(work_full, 1)

            def tokens_t(b):
                bank = claim(("Y", b, 0))
                pe.wait_ge(y_ready, TB * (b + 1))
                for k in range(KD):
                    for t in range(TB):
                        tr = pe.transpose(ps[:, bank, (TB * k + t) * P:(TB * k + t + 1) * P],
                                          y[:, TB * b + t, k * P:(k + 1) * P], ident[:, :])
                tr.then_inc(work_full, 1)

            def router_logits(part):
                lo, hi = PARTS[part]
                bank = claim(("L", part, 0))
                pe.wait_ge(*emptied[slot_of[("Y", (hi - 1) // TB, 0)]])
                for i in range(lo, hi):
                    for k in range(KD):
                        for half in (y_hi, y_lo):
                            mm = pe.matmul(ps[:, bank, (i - lo) * 2 * E:(i - lo + 1) * 2 * E],
                                           half[:, k, i * P:(i + 1) * P], wr_t[:, k, :],
                                           start=(k == 0 and half is y_hi), stop=(k == KD - 1 and half is y_lo))
                mm.then_inc(work_full, 1)

            def scores_tr(part, n):
                bank = claim(("R", part, n))
                pe.wait_ge(score_ready, part + 1)
                for j, i in enumerate(range(*PARTS[part])):
                    tr = pe.transpose(ps[:, bank, j * P:(j + 1) * P], score_st[:, i, :].bitcast(F32), ident[:, :])
                tr.then_inc(work_full, 1)

            pe.wait_ge(consts, 1)
            for _ in range(WARM_UP):
                pe.transpose(ps[:, SCORE[0], 0:P], ident[:, :], ident[:, :])
            pe.wait_ge(small_in, 96)
            for k in range(KD):
                pe.transpose(ps[:, 7, k * E:(k + 1) * E], wr_sb[:, k * P:(k + 1) * P], ident[0:E, 0:E])
            for g in range(2):
                for f in range(FD):
                    at = KD * E + (g * FD + f) * E
                    tr = pe.transpose(ps[:, 7, at:at + E], bgu_sb[:, 2 * f * P + g:2 * (f + 1) * P:2],
                                      ident[0:E, 0:E])
            tr.then_inc(small_t, 1)
            for kind, b, n in steps:
                if kind == "T":
                    stacks_t(b, n)
                elif kind == "X":
                    row_scores(b, n)
                elif kind == "M":
                    maxima_t(b, n)
                elif kind == "S":
                    scores(b, n)
                elif kind == "V":
                    weigh(b, n)
                elif kind == "O":
                    output(b, n)
                elif kind == "Y":
                    tokens_t(b)
                elif kind == "L":
                    router_logits(b)
                elif kind == "R":
                    scores_tr(b, n)

            def gate_up(e, par, c):
                n = CH * e + c
                tg, f = c // FD, c % FD
                b0 = 2 * (c % 2)
                fwait(pe, u_ready, n - 1)
                if c == 0:
                    pe.wait_ge(w_hi, 2 * e + 1)
                    pe.wait_ge(w_lo, 3 * e + 2)
                tok = slice(tg * GRP, (tg + 1) * GRP)
                for g in range(2):
                    for k in range(KD):
                        hi = gu_hi[:, par, k, g, f * P:(f + 1) * P]
                        lo = gu_lo[:, par, k, g, f * P:(f + 1) * P]
                        o = ps[:, b0 + g, :]
                        pe.matmul(o, hi, y_hi[:, k, tok], start=(k == 0), stop=False)
                        pe.matmul(o, hi, y_lo[:, k, tok], start=False, stop=False)
                        mm = pe.matmul(o, lo, y_hi[:, k, tok], start=False, stop=(k == KD - 1))
                mm.then_inc(gu_done, 1)

            def down(n, e, par, c):
                tg, f = c // FD, c % FD
                pe.wait_ge(hlo_ready, n + 1)
                pe.wait_ge(w_lo, 3 * e + 3)
                for m in range(KD):
                    hi = dn_hi[:, par, f, m * P:(m + 1) * P]
                    lo = dn_lo[:, par, f, m * P:(m + 1) * P]
                    o = ps[:, acc_bank(tg, m), :]
                    pe.matmul(o, hi, h_hi[:, c, :], start=False, stop=True, skip_group_check=True)
                    pe.matmul(o, hi, h_lo[:, c, :], start=False, stop=True, skip_group_check=True)
                    mm = pe.matmul(o, lo, h_hi[:, c, :], start=False, stop=True, skip_group_check=True)
                mm.then_inc(dn_done, 1)

            def select_scores():
                pe.wait_ge(consts, 17)
                pe.wait_ge(score_sT_ready, 2)
                pe.wait_ge(*emptied[slot_of[("R", 1, 0)]])
                for e in range(2):
                    pe.matmul(ps[:, acc_bank(1, e), :], sel[:, e, :], score_sT[:, GRP:T], start=True, stop=True
                              ).then_inc(sel_full, 1)

            def bias_terms(tg):
                for m in range(KD):
                    pe.matmul(ps[:, acc_bank(tg, m), :], bdn_st[:, m * P:(m + 1) * P],
                              score_sT[:, tg * GRP:(tg + 1) * GRP], start=True, stop=True, skip_group_check=True)

            def expert(e, par, first, second):
                for c in range(CH):
                    n = CH * e + c
                    if first and c == 0:
                        pe.wait_ge(exp_done, 2 * B * UNITS)
                    if first and c == 2:
                        router_logits(1)
                    gate_up(e, par, c)
                    if first and c == 1:
                        tokens_t(B - 1)
                        pe.wait_ge(score_sT_ready, 1)
                        pe.wait_ge(*emptied[attention_last[6]])
                        pe.wait_ge(o_evac, 2 * B)
                        bias_terms(0)
                    if first and c == 3:
                        down(0, 0, 0, 0)
                        scores_tr(1, 0)
                        select_scores()
                    if second and c == 0:
                        down(1, 0, 0, 1)
                        pe.wait_ge(score_sel, 2)
                        bias_terms(1)
                    if c >= 2 and not first:
                        down(n - 2, e, par, c - 2)
                    elif not first:
                        down(n - 2, e - 1, 1 - par, c + 2)

            expert(0, 0, True, False)
            expert(1, 1, False, True)
            with pe.Fori(1, E // 2) as i:
                expert(2 * i, 0, False, False)
                expert(2 * i + 1, 1, False, False)
            down(CH * E - 2, E - 1, 1, 2)

            def outputs_back(j):
                tg = j // 2
                pe.wait_ge(u_ready, CH * E)
                pe.wait_ge(outt_ready[0], tg + 1)
                pe.wait_ge(outt_ready[1], tg + 1)
                for a in range(2):
                    for m in range(KD):
                        col = ((2 * j + a) % 4) * P
                        tr = pe.transpose(ps[:, j, (a * KD + m) * P:(a * KD + m + 1) * P],
                                          out_t[:, tg, m, col:col + P], ident[:, :])
                tr.then_inc(out_tr, 1)

            outputs_back(0)
            down(CH * E - 1, E - 1, 1, 3)
            outputs_back(1)
            outputs_back(2)
            outputs_back(3)


_INS = ['x', 'ctx_2048', 'L0_ffn_router_weight', 'L0_ffn_router_bias', 'L0_ffn_gate_up_proj',
        'L0_ffn_gate_up_proj_bias', 'L0_ffn_down_proj', 'L0_ffn_down_proj_bias']


def kernel(**inputs):
    import numpy as _np
    import concourse.bacc as _bacc
    from concourse import mybir as _mybir
    from concourse.bass_utils import run_bass_kernel_spmd as _run

    nc = _bacc.Bacc("TRN2", target_bir_lowering=False, num_devices=1)
    arrays, args = {}, []
    for name in _INS:
        a = _np.ascontiguousarray(inputs[name])
        arrays[f"in_{name}_dram"] = a
        args.append(nc.dram_tensor(f"in_{name}_dram", a.shape, _mybir.dt.from_np(a.dtype), kind="ExternalInput").ap())
    tokens = args[0].shape[0] * args[0].shape[1]
    scores = nc.dram_tensor("scores_dram", (args[2].shape[0], tokens), _mybir.dt.float32, kind="Internal").ap()
    out = nc.dram_tensor("out_0_dram", args[0].shape, _mybir.dt.float32, kind="ExternalOutput").ap()
    xattn_moe(nc, *args, scores, out)
    r = _run(nc, [arrays], core_ids=[0])
    return r.results[0]["out_0_dram"]
```
